# Optimizing a Trainium2 kernel written in Bass

```python
import numpy as np
import jax
import jax.numpy as jnp

def _softmax(x, axis=-1):
    return jax.nn.softmax(x, axis=axis)
def _gelu(x):
    return jax.nn.gelu(x, approximate=True)
def _silu(x):
    return jax.nn.silu(x)
def _sigmoid(x):
    return jax.nn.sigmoid(x)
def _layernorm(x, axis=-1, eps=1e-5):
    m = jnp.mean(x, axis=axis, keepdims=True)
    v = jnp.var(x, axis=axis, keepdims=True)
    return (x - m) / jnp.sqrt(v + eps)
def _scatter_add(tgt, idx, src, axis=0):
    return tgt.at[idx].add(src)
def _segment_sum(src, seg, n):
    return jax.ops.segment_sum(src, seg, n)

kernel_name = 'mk_conv_preact_d4_conv_nhwc256_0eda12'

def setup_inputs(seed: int = 0):
    np.random.seed(seed)
    _w = jnp.asarray
    def _rec_inputs():
        import jax
        import jax.numpy as jnp
        _gk = jax.random.key(seed)
        x = -0.0005207 + 1.001 * jax.random.normal(jax.random.fold_in(_gk, 1), (8, 32, 32, 256), jnp.float32)
        return x
    x = _rec_inputs()
    def _L0_conv_setup():
        import jax, jax.numpy as jnp
        import numpy as np
        B, N1, N2, E = (8, 32, 32, 256)
        H = 8
        KD = E // H
        HD = E // H
        L = N1 * N2
        SCALING = KD ** (-0.5)
        LN_EPS = 1e-05

        def _rel_pos_2d():
            half = 1.0 / 10000.0 ** jnp.linspace(0.0, 1.0, KD // 2)
            angle = jnp.repeat(half, 2)
            decay = jnp.log(1.0 - 2.0 ** (-2.0 - 5.0 * jnp.arange(H, dtype=jnp.float32) / H))
            i1 = jnp.arange(N1, dtype=jnp.float32)
            i2 = jnp.arange(N2, dtype=jnp.float32)
            index_k = (i1[:, None] + i2[None, :]).reshape(L)
            sin_k = jnp.sin(index_k[:, None] * angle[None, :])
            cos_k = jnp.cos(index_k[:, None] * angle[None, :])
            sin_q = sin_k[None, None]
            cos_q = cos_k[None, None]
            d = (jnp.abs(i1[:, None, None, None] - i1[None, None, :, None]) + jnp.abs(i2[None, :, None, None] - i2[None, None, None, :])).reshape(L, L)
            mask = jnp.exp(d[None, :, :] * decay[:, None, None])
            mask = jnp.nan_to_num(mask)
            mask = mask / jnp.sqrt(mask.sum(-1, keepdims=True))
            return (sin_q, cos_q, sin_k, cos_k, mask)

        def rotate_every_two(x):
            x1 = x[..., ::2]
            x2 = x[..., 1::2]
            return jnp.stack((-x2, x1), axis=-1).reshape(x.shape)

        def theta_shift(x, sin, cos):
            return x * cos + rotate_every_two(x) * sin
        key = jax.random.key(seed)
        ks = jax.random.split(key, 5)
        gain_qkv = 2.0 ** (-2.5) * (6.0 / (E + E)) ** 0.5
        gain_o = 2.0 ** (-1) * (6.0 / (E + E)) ** 0.5
        x = jax.random.normal(ks[0], (B, N1, N2, E), dtype=jnp.float32)
        Wq = jax.random.uniform(ks[1], (E, E), jnp.float32, -gain_qkv, gain_qkv)
        Wk = jax.random.uniform(ks[2], (E, E), jnp.float32, -gain_qkv, gain_qkv)
        Wv = jax.random.uniform(ks[3], (E, E), jnp.float32, -gain_qkv, gain_qkv)
        Wo = jax.random.uniform(ks[4], (E, E), jnp.float32, -gain_o, gain_o)
        ln_g = jnp.ones((HD,), jnp.float32)
        ln_b = jnp.zeros((HD,), jnp.float32)
        return {'x': x, 'Wq': Wq, 'Wk': Wk, 'Wv': Wv, 'Wo': Wo, 'ln_g': ln_g, 'ln_b': ln_b}
    _L0_conv_all = _L0_conv_setup()
    _L0_conv_in = {k: v for k, v in _L0_conv_all.items() if k in ('Wq', 'Wk', 'Wv', 'Wo', 'ln_g', 'ln_b', )}
    del _L0_conv_all

    def _L1_conv_setup():
        import jax, jax.numpy as jnp
        import numpy as np
        DIM = 256
        INNER = 512
        NH = 8
        DH = INNER // NH
        NB = INNER // 4
        BS = 4
        K = 4
        EPS = 1e-06
        LN_EPS = 1e-05

        def _mlstm_forward(x, W_up, conv_w, conv_b, Wq, Wk, Wv, W_i, b_i, W_f, b_f, norm_w, skip, W_down):
            B, H, W, C = x.shape
            S = H * W
            xs = x.reshape(B, S, C)
            up = xs @ W_up.T
            x_m, z = (up[..., :INNER], up[..., INNER:])
            xp = jnp.pad(x_m, ((0, 0), (K - 1, 0), (0, 0)))
            x_conv = conv_b + sum((xp[:, k:k + S, :] * conv_w[:, 0, k] for k in range(K)))
            x_act = jax.nn.silu(x_conv)
            xa = x_act.reshape(B, S, NB, BS)
            q = jnp.einsum('bsnd,nod->bsno', xa, Wq).reshape(B, S, INNER)
            k = jnp.einsum('bsnd,nod->bsno', xa, Wk).reshape(B, S, INNER)
            xv = x_m.reshape(B, S, NB, BS)
            v = jnp.einsum('bsnd,nod->bsno', xv, Wv).reshape(B, S, INNER)
            gate_in = jnp.concatenate([q, k, v], axis=-1)
            ig = (gate_in @ W_i.T + b_i).transpose(0, 2, 1)
            fg = (gate_in @ W_f.T + b_f).transpose(0, 2, 1)
            qh = q.reshape(B, S, NH, DH).transpose(0, 2, 1, 3)
            kh = k.reshape(B, S, NH, DH).transpose(0, 2, 1, 3) / np.sqrt(DH)
            vh = v.reshape(B, S, NH, DH).transpose(0, 2, 1, 3)
            lf = jax.nn.log_sigmoid(fg)
            lc = jnp.cumsum(lf, axis=-1)
            M = lc[..., :, None] - lc[..., None, :]
            mask = jnp.tril(jnp.ones((S, S), dtype=bool))
            logD = jnp.where(mask, M + ig[..., None, :], -jnp.inf)
            m = jnp.max(logD, axis=-1, keepdims=True)
            D = jnp.exp(logD - m)
            Cmat = jnp.einsum('bhid,bhjd->bhij', qh, kh) * D
            norm = jnp.maximum(jnp.abs(Cmat.sum(-1, keepdims=True)), jnp.exp(-m))
            h_cell = jnp.einsum('bhij,bhjd->bhid', Cmat / (norm + EPS), vh)
            mu = h_cell.mean(-1, keepdims=True)
            var = h_cell.var(-1, keepdims=True)
            hn = (h_cell - mu) / jnp.sqrt(var + LN_EPS)
            hn = hn * norm_w.reshape(NH, 1, DH)
            h = hn.transpose(0, 2, 1, 3).reshape(B, S, INNER)
            h = h + skip * x_act
            h = h * jax.nn.silu(z)
            out = h @ W_down.T
            return out.reshape(B, H, W, C)
        key = jax.random.key(seed)
        ks = jax.random.split(key, 14)
        f32 = jnp.float32
        return {'x': jax.random.normal(ks[0], (4, 32, 32, DIM), f32), 'W_up': jax.random.normal(ks[1], (2 * INNER, DIM), f32) * 0.05, 'conv_w': jax.random.normal(ks[2], (INNER, 1, K), f32) * 0.3, 'conv_b': jax.random.normal(ks[3], (INNER,), f32) * 0.05, 'Wq': jax.random.normal(ks[4], (NB, BS, BS), f32) * 0.3, 'Wk': jax.random.normal(ks[5], (NB, BS, BS), f32) * 0.3, 'Wv': jax.random.normal(ks[6], (NB, BS, BS), f32) * 0.3, 'W_i': jax.random.normal(ks[7], (NH, 3 * INNER), f32) * 0.02, 'b_i': jax.random.normal(ks[8], (NH,), f32) * 0.1, 'W_f': jax.random.normal(ks[9], (NH, 3 * INNER), f32) * 0.02, 'b_f': jax.random.normal(ks[10], (NH,), f32) * 0.1, 'norm_w': jnp.ones((INNER,), f32), 'skip': jax.random.normal(ks[11], (INNER,), f32) * 0.1, 'W_down': jax.random.normal(ks[12], (DIM, INNER), f32) * 0.05}
    _L1_conv_all = _L1_conv_setup()
    _L1_conv_in = {k: v for k, v in _L1_conv_all.items() if k in ('W_up', 'conv_w', 'conv_b', 'Wq', 'Wk', 'Wv', 'W_i', 'b_i', 'W_f', 'b_f', 'norm_w', 'skip', 'W_down', )}
    del _L1_conv_all

    def _L2_conv_setup():
        import jax, jax.numpy as jnp
        import numpy as np
        B, H, W, C = (1, 64, 64, 256)
        NH = 8
        K = 7

        def _neighbor_idx(n, k):
            start = jnp.clip(jnp.arange(n) - k // 2, 0, n - k)
            return start[:, None] + jnp.arange(k)[None, :]
        key = jax.random.key(seed)
        ks = jax.random.split(key, 6)
        x = jax.random.normal(ks[0], (B, H, W, C), dtype=jnp.float32)
        qkv_w = jax.random.normal(ks[1], (3 * C, C), dtype=jnp.float32) * 0.02
        qkv_b = jnp.zeros((3 * C,), dtype=jnp.float32)
        proj_w = jax.random.normal(ks[2], (C, C), dtype=jnp.float32) * 0.02
        proj_b = jnp.zeros((C,), dtype=jnp.float32)
        rpb = jax.random.normal(ks[3], (NH, 2 * K - 1, 2 * K - 1), dtype=jnp.float32) * 0.02
        return {'x': x, 'qkv_w': qkv_w, 'qkv_b': qkv_b, 'proj_w': proj_w, 'proj_b': proj_b, 'rpb': rpb}
    _L2_conv_all = _L2_conv_setup()
    _L2_conv_in = {k: v for k, v in _L2_conv_all.items() if k in ('qkv_w', 'qkv_b', 'proj_w', 'proj_b', 'rpb', )}
    del _L2_conv_all

    def _L3_conv_setup():
        import jax, jax.numpy as jnp
        import numpy as np
        EMBED_DIM = 256
        NUM_CH = 8
        CH_DIM = EMBED_DIM // NUM_CH
        K = 7
        PAD = K // 2
        WIN = K * K
        EPS = 1e-06

        def rms_norm(x, w):
            return x / jnp.sqrt(jnp.mean(x * x, axis=-1, keepdims=True) + EPS) * w

        def apply_rope(x):
            D = x.shape[-1]
            half = D // 2
            pos = jnp.arange(x.shape[-2], dtype=jnp.float32)
            freqs = 1.0 / 10000.0 ** (jnp.arange(half, dtype=x.dtype) / half)
            angles = pos[:, None] * freqs
            cos, sin = (jnp.cos(angles), jnp.sin(angles))
            x1, x2 = (x[..., :half], x[..., half:2 * half])
            return jnp.concatenate([x1 * cos - x2 * sin, x1 * sin + x2 * cos], axis=-1)

        def rel_dist_flat():
            c = np.arange(K, dtype=np.float32) - K // 2
            gy, gx = np.meshgrid(c, c, indexing='ij')
            return jnp.asarray(np.sqrt(gy ** 2 + gx ** 2).reshape(-1))

        def unfold2d(t):
            B, Hs, Ws, C = t.shape
            tp = jnp.pad(t, ((0, 0), (PAD, PAD), (PAD, PAD), (0, 0)))
            wins = [tp[:, i:i + Hs, j:j + Ws, :] for i in range(K) for j in range(K)]
            return jnp.stack(wins, axis=3)
        key = jax.random.key(seed)
        ks = jax.random.split(key, 8)
        B, Hs, Ws, C = (2, 64, 64, EMBED_DIM)
        s = 0.02
        return {'x': jax.random.normal(ks[0], (B, Hs, Ws, C), dtype=jnp.float32), 'w_qkv': jax.random.normal(ks[1], (3 * C, C), dtype=jnp.float32) * s, 'w_qn': jnp.ones((CH_DIM,), dtype=jnp.float32), 'w_kn': jnp.ones((CH_DIM,), dtype=jnp.float32), 'w_wp': jax.random.normal(ks[2], (2 * NUM_CH, C), dtype=jnp.float32) * s, 'b_wp': jax.random.normal(ks[3], (2 * NUM_CH,), dtype=jnp.float32) * s, 'w_on': jnp.ones((C,), dtype=jnp.float32), 'w_out': jax.random.normal(ks[4], (C, C), dtype=jnp.float32) * s}
    _L3_conv_all = _L3_conv_setup()
    _L3_conv_in = {k: v for k, v in _L3_conv_all.items() if k in ('w_qkv', 'w_qn', 'w_kn', 'w_wp', 'b_wp', 'w_on', 'w_out', )}
    del _L3_conv_all

    return {
        "x": x,
        "L0_conv_Wq": _L0_conv_in["Wq"],
        "L0_conv_Wk": _L0_conv_in["Wk"],
        "L0_conv_Wv": _L0_conv_in["Wv"],
        "L0_conv_Wo": _L0_conv_in["Wo"],
        "L0_conv_ln_g": _L0_conv_in["ln_g"],
        "L0_conv_ln_b": _L0_conv_in["ln_b"],
        "L1_conv_W_up": _L1_conv_in["W_up"],
        "L1_conv_conv_w": _L1_conv_in["conv_w"],
        "L1_conv_conv_b": _L1_conv_in["conv_b"],
        "L1_conv_Wq": _L1_conv_in["Wq"],
        "L1_conv_Wk": _L1_conv_in["Wk"],
        "L1_conv_Wv": _L1_conv_in["Wv"],
        "L1_conv_W_i": _L1_conv_in["W_i"],
        "L1_conv_b_i": _L1_conv_in["b_i"],
        "L1_conv_W_f": _L1_conv_in["W_f"],
        "L1_conv_b_f": _L1_conv_in["b_f"],
        "L1_conv_norm_w": _L1_conv_in["norm_w"],
        "L1_conv_skip": _L1_conv_in["skip"],
        "L1_conv_W_down": _L1_conv_in["W_down"],
        "L2_conv_qkv_w": _L2_conv_in["qkv_w"],
        "L2_conv_qkv_b": _L2_conv_in["qkv_b"],
        "L2_conv_proj_w": _L2_conv_in["proj_w"],
        "L2_conv_proj_b": _L2_conv_in["proj_b"],
        "L2_conv_rpb": _L2_conv_in["rpb"],
        "L3_conv_w_qkv": _L3_conv_in["w_qkv"],
        "L3_conv_w_qn": _L3_conv_in["w_qn"],
        "L3_conv_w_kn": _L3_conv_in["w_kn"],
        "L3_conv_w_wp": _L3_conv_in["w_wp"],
        "L3_conv_b_wp": _L3_conv_in["b_wp"],
        "L3_conv_w_on": _L3_conv_in["w_on"],
        "L3_conv_w_out": _L3_conv_in["w_out"],
    }

def reference(x, L0_conv_Wq, L0_conv_Wk, L0_conv_Wv, L0_conv_Wo, L0_conv_ln_g, L0_conv_ln_b, L1_conv_W_up, L1_conv_conv_w, L1_conv_conv_b, L1_conv_Wq, L1_conv_Wk, L1_conv_Wv, L1_conv_W_i, L1_conv_b_i, L1_conv_W_f, L1_conv_b_f, L1_conv_norm_w, L1_conv_skip, L1_conv_W_down, L2_conv_qkv_w, L2_conv_qkv_b, L2_conv_proj_w, L2_conv_proj_b, L2_conv_rpb, L3_conv_w_qkv, L3_conv_w_qn, L3_conv_w_kn, L3_conv_w_wp, L3_conv_b_wp, L3_conv_w_on, L3_conv_w_out):
    import jax
    import jax.numpy as jnp
    def _L0_conv_ref(x, Wq, Wk, Wv, Wo, ln_g, ln_b):
        import jax, jax.numpy as jnp
        import numpy as np
        B, N1, N2, E = (8, 32, 32, 256)
        H = 8
        KD = E // H
        HD = E // H
        L = N1 * N2
        SCALING = KD ** (-0.5)
        LN_EPS = 1e-05

        def _rel_pos_2d():
            half = 1.0 / 10000.0 ** jnp.linspace(0.0, 1.0, KD // 2)
            angle = jnp.repeat(half, 2)
            decay = jnp.log(1.0 - 2.0 ** (-2.0 - 5.0 * jnp.arange(H, dtype=jnp.float32) / H))
            i1 = jnp.arange(N1, dtype=jnp.float32)
            i2 = jnp.arange(N2, dtype=jnp.float32)
            index_k = (i1[:, None] + i2[None, :]).reshape(L)
            sin_k = jnp.sin(index_k[:, None] * angle[None, :])
            cos_k = jnp.cos(index_k[:, None] * angle[None, :])
            sin_q = sin_k[None, None]
            cos_q = cos_k[None, None]
            d = (jnp.abs(i1[:, None, None, None] - i1[None, None, :, None]) + jnp.abs(i2[None, :, None, None] - i2[None, None, None, :])).reshape(L, L)
            mask = jnp.exp(d[None, :, :] * decay[:, None, None])
            mask = jnp.nan_to_num(mask)
            mask = mask / jnp.sqrt(mask.sum(-1, keepdims=True))
            return (sin_q, cos_q, sin_k, cos_k, mask)

        def rotate_every_two(x):
            x1 = x[..., ::2]
            x2 = x[..., 1::2]
            return jnp.stack((-x2, x1), axis=-1).reshape(x.shape)

        def theta_shift(x, sin, cos):
            return x * cos + rotate_every_two(x) * sin
        sin_q, cos_q, sin_k, cos_k, mask = _rel_pos_2d()
        xf = x.reshape(B, L, E)
        q = (xf @ Wq.T).reshape(B, L, H, KD).transpose(0, 2, 1, 3)
        k = (xf @ Wk.T * SCALING).reshape(B, L, H, KD).transpose(0, 2, 1, 3)
        vr = (xf @ Wv.T).reshape(B, L, H, HD).transpose(0, 2, 1, 3)
        qr = theta_shift(q, sin_q, cos_q)
        kr = theta_shift(k, sin_k[None, None], cos_k[None, None])
        qk = jnp.einsum('bhqd,bhkd->bhqk', qr, kr) * mask[None]
        den = jnp.clip(jax.lax.stop_gradient(jnp.abs(qk)).sum(-1, keepdims=True), 1.0, 50000.0)
        qk = qk / den
        out = jnp.einsum('bhqk,bhkd->bhqd', qk, vr).transpose(0, 2, 1, 3)
        mu = out.mean(-1, keepdims=True)
        var = out.var(-1, keepdims=True)
        out = (out - mu) / jnp.sqrt(var + LN_EPS) * ln_g + ln_b
        out = jax.nn.gelu(out.reshape(B, L, H * HD), approximate=False)
        out = out @ Wo.T
        return out.reshape(B, N1, N2, E)

    def _L1_conv_ref(x, W_up, conv_w, conv_b, Wq, Wk, Wv, W_i, b_i, W_f, b_f, norm_w, skip, W_down):
        import jax, jax.numpy as jnp
        import numpy as np
        DIM = 256
        INNER = 512
        NH = 8
        DH = INNER // NH
        NB = INNER // 4
        BS = 4
        K = 4
        EPS = 1e-06
        LN_EPS = 1e-05

        def _mlstm_forward(x, W_up, conv_w, conv_b, Wq, Wk, Wv, W_i, b_i, W_f, b_f, norm_w, skip, W_down):
            B, H, W, C = x.shape
            S = H * W
            xs = x.reshape(B, S, C)
            up = xs @ W_up.T
            x_m, z = (up[..., :INNER], up[..., INNER:])
            xp = jnp.pad(x_m, ((0, 0), (K - 1, 0), (0, 0)))
            x_conv = conv_b + sum((xp[:, k:k + S, :] * conv_w[:, 0, k] for k in range(K)))
            x_act = jax.nn.silu(x_conv)
            xa = x_act.reshape(B, S, NB, BS)
            q = jnp.einsum('bsnd,nod->bsno', xa, Wq).reshape(B, S, INNER)
            k = jnp.einsum('bsnd,nod->bsno', xa, Wk).reshape(B, S, INNER)
            xv = x_m.reshape(B, S, NB, BS)
            v = jnp.einsum('bsnd,nod->bsno', xv, Wv).reshape(B, S, INNER)
            gate_in = jnp.concatenate([q, k, v], axis=-1)
            ig = (gate_in @ W_i.T + b_i).transpose(0, 2, 1)
            fg = (gate_in @ W_f.T + b_f).transpose(0, 2, 1)
            qh = q.reshape(B, S, NH, DH).transpose(0, 2, 1, 3)
            kh = k.reshape(B, S, NH, DH).transpose(0, 2, 1, 3) / np.sqrt(DH)
            vh = v.reshape(B, S, NH, DH).transpose(0, 2, 1, 3)
            lf = jax.nn.log_sigmoid(fg)
            lc = jnp.cumsum(lf, axis=-1)
            M = lc[..., :, None] - lc[..., None, :]
            mask = jnp.tril(jnp.ones((S, S), dtype=bool))
            logD = jnp.where(mask, M + ig[..., None, :], -jnp.inf)
            m = jnp.max(logD, axis=-1, keepdims=True)
            D = jnp.exp(logD - m)
            Cmat = jnp.einsum('bhid,bhjd->bhij', qh, kh) * D
            norm = jnp.maximum(jnp.abs(Cmat.sum(-1, keepdims=True)), jnp.exp(-m))
            h_cell = jnp.einsum('bhij,bhjd->bhid', Cmat / (norm + EPS), vh)
            mu = h_cell.mean(-1, keepdims=True)
            var = h_cell.var(-1, keepdims=True)
            hn = (h_cell - mu) / jnp.sqrt(var + LN_EPS)
            hn = hn * norm_w.reshape(NH, 1, DH)
            h = hn.transpose(0, 2, 1, 3).reshape(B, S, INNER)
            h = h + skip * x_act
            h = h * jax.nn.silu(z)
            out = h @ W_down.T
            return out.reshape(B, H, W, C)
        return _mlstm_forward(x, W_up, conv_w, conv_b, Wq, Wk, Wv, W_i, b_i, W_f, b_f, norm_w, skip, W_down)

    def _L2_conv_ref(x, qkv_w, qkv_b, proj_w, proj_b, rpb):
        import jax, jax.numpy as jnp
        import numpy as np
        B, H, W, C = (1, 64, 64, 256)
        NH = 8
        K = 7

        def _neighbor_idx(n, k):
            start = jnp.clip(jnp.arange(n) - k // 2, 0, n - k)
            return start[:, None] + jnp.arange(k)[None, :]
        b, h, w, c = x.shape
        nh = rpb.shape[0]
        k = (rpb.shape[1] + 1) // 2
        hd = c // nh
        scale = hd ** (-0.5)
        qkv = x @ qkv_w.T + qkv_b
        qkv = qkv.reshape(b, h, w, 3, nh, hd)
        qkv = jnp.transpose(qkv, (3, 0, 4, 1, 2, 5))
        q, kk, v = (qkv[0], qkv[1], qkv[2])
        ni = _neighbor_idx(h, k)
        nj = _neighbor_idx(w, k)
        k_nb = kk[:, :, ni][:, :, :, :, nj]
        v_nb = v[:, :, ni][:, :, :, :, nj]
        attn = jnp.einsum('bnijd,bniajcd->bnijac', q * scale, k_nb)
        bi = ni - jnp.arange(h)[:, None] + (k - 1)
        bj = nj - jnp.arange(w)[:, None] + (k - 1)
        bias = rpb[:, bi][:, :, :, bj]
        attn = attn + jnp.transpose(bias, (0, 1, 3, 2, 4))[None]
        attn = jax.nn.softmax(attn.reshape(b, nh, h, w, k * k), axis=-1)
        attn = attn.reshape(b, nh, h, w, k, k)
        out = jnp.einsum('bnijac,bniajcd->bnijd', attn, v_nb)
        out = jnp.transpose(out, (0, 2, 3, 1, 4)).reshape(b, h, w, c)
        out = out @ proj_w.T + proj_b
        return out

    def _L3_conv_ref(x, w_qkv, w_qn, w_kn, w_wp, b_wp, w_on, w_out):
        import jax, jax.numpy as jnp
        import numpy as np
        EMBED_DIM = 256
        NUM_CH = 8
        CH_DIM = EMBED_DIM // NUM_CH
        K = 7
        PAD = K // 2
        WIN = K * K
        EPS = 1e-06

        def rms_norm(x, w):
            return x / jnp.sqrt(jnp.mean(x * x, axis=-1, keepdims=True) + EPS) * w

        def apply_rope(x):
            D = x.shape[-1]
            half = D // 2
            pos = jnp.arange(x.shape[-2], dtype=jnp.float32)
            freqs = 1.0 / 10000.0 ** (jnp.arange(half, dtype=x.dtype) / half)
            angles = pos[:, None] * freqs
            cos, sin = (jnp.cos(angles), jnp.sin(angles))
            x1, x2 = (x[..., :half], x[..., half:2 * half])
            return jnp.concatenate([x1 * cos - x2 * sin, x1 * sin + x2 * cos], axis=-1)

        def rel_dist_flat():
            c = np.arange(K, dtype=np.float32) - K // 2
            gy, gx = np.meshgrid(c, c, indexing='ij')
            return jnp.asarray(np.sqrt(gy ** 2 + gx ** 2).reshape(-1))

        def unfold2d(t):
            B, Hs, Ws, C = t.shape
            tp = jnp.pad(t, ((0, 0), (PAD, PAD), (PAD, PAD), (0, 0)))
            wins = [tp[:, i:i + Hs, j:j + Ws, :] for i in range(K) for j in range(K)]
            return jnp.stack(wins, axis=3)
        B, Hs, Ws, C = x.shape
        H, D = (NUM_CH, CH_DIM)
        L = Hs * Ws
        rel_dist = rel_dist_flat()
        max_dist = float(np.sqrt(2.0) * (K // 2))
        qkv = jax.nn.silu(x @ w_qkv.T)
        q, k, v = jnp.split(qkv, 3, axis=-1)
        q_flat = apply_rope(rms_norm(q.reshape(B, L, H, D), w_qn))
        k_flat = apply_rope(rms_norm(k.reshape(B, L, H, D), w_kn))
        k_sp = k_flat.reshape(B, Hs, Ws, C)
        wp = jax.nn.silu(x @ w_wp.T + b_wp)
        width_raw, sharp_raw = jnp.split(wp, 2, axis=-1)
        width = jax.nn.sigmoid(width_raw) * max_dist + 0.5
        sharp = jax.nn.sigmoid(sharp_raw) * 9.5 + 0.5
        k_win = unfold2d(k_sp).reshape(B, L, WIN, H, D)
        v_win = unfold2d(v).reshape(B, L, WIN, H, D)
        scale = D ** (-0.5)
        scores = jnp.einsum('blhd,blwhd->blhw', q_flat, k_win) * scale
        soft_mask = jax.nn.sigmoid((width.reshape(B, L, H, 1) - rel_dist) * sharp.reshape(B, L, H, 1))
        scores = scores - (1.0 - soft_mask) * 10000.0
        attn = jax.nn.softmax(scores, axis=-1)
        out = jnp.einsum('blhw,blwhd->blhd', attn, v_win).reshape(B, Hs, Ws, C)
        out = rms_norm(out, w_on)
        return jax.nn.silu((out + v) @ w_out.T)

    def _gn(v, G=32, eps=1e-5):
        B_, H_, W_, C_ = v.shape
        g = v.reshape(B_, H_, W_, G, C_ // G)
        m = jnp.mean(g, axis=(1, 2, 4), keepdims=True)
        s = jnp.var(g, axis=(1, 2, 4), keepdims=True)
        return ((g - m) / jnp.sqrt(s + eps)).reshape(v.shape)

    def _ln_c(v, eps=1e-6):
        m = jnp.mean(v, axis=-1, keepdims=True)
        s = jnp.var(v, axis=-1, keepdims=True)
        return (v - m) / jnp.sqrt(s + eps)

    def _ln_t(v, eps=1e-5):
        m = jnp.mean(v, axis=-1, keepdims=True)
        s = jnp.var(v, axis=-1, keepdims=True)
        return (v - m) / jnp.sqrt(s + eps)

    def _to_tokens(v):
        B_, H_, W_, C_ = v.shape
        return v.reshape(B_, H_ * W_, C_)
    def _from_tokens(t, like):
        return t.reshape(like.shape)

    x = x + _L0_conv_ref(_gn(x), L0_conv_Wq, L0_conv_Wk, L0_conv_Wv, L0_conv_Wo, L0_conv_ln_g, L0_conv_ln_b)
    x = x + _L1_conv_ref(_gn(x), L1_conv_W_up, L1_conv_conv_w, L1_conv_conv_b, L1_conv_Wq, L1_conv_Wk, L1_conv_Wv, L1_conv_W_i, L1_conv_b_i, L1_conv_W_f, L1_conv_b_f, L1_conv_norm_w, L1_conv_skip, L1_conv_W_down)
    x = x + _L2_conv_ref(_gn(x), L2_conv_qkv_w, L2_conv_qkv_b, L2_conv_proj_w, L2_conv_proj_b, L2_conv_rpb)
    x = x + _L3_conv_ref(_gn(x), L3_conv_w_qkv, L3_conv_w_qn, L3_conv_w_kn, L3_conv_w_wp, L3_conv_b_wp, L3_conv_w_on, L3_conv_w_out)
    return x


_drawn_inputs = setup_inputs


def setup_inputs(seed=0):
    import zlib

    import numpy as np

    out = dict(_drawn_inputs(seed))
    spreads = {'L0_conv_ln_g': (1.0, 0.2),
     'L0_conv_ln_b': (0.0, 0.1),
     'L1_conv_norm_w': (1.0, 0.2),
     'L2_conv_qkv_b': (0.0, 0.279),
     'L2_conv_proj_b': (0.0, 0.1),
     'L3_conv_w_qn': (1.0, 0.6),
     'L3_conv_w_kn': (1.0, 0.6),
     'L3_conv_w_on': (1.0, 0.553)}
    factors = {'L1_conv_b_i': 5.221,
     'L1_conv_b_f': 5.546,
     'L1_conv_skip': 4.533,
     'L2_conv_qkv_w': 3.503,
     'L2_conv_rpb': 38.49,
     'L3_conv_b_wp': 7.662}
    for name, (base, spread) in spreads.items():
        noise = np.random.default_rng([zlib.crc32(name.encode()), seed]).standard_normal(out[name].shape)
        drawn = base * np.exp(spread * noise) if base else spread * noise
        out[name] = jnp.asarray(drawn.astype(out[name].dtype))
    for name, factor in factors.items():
        out[name] = (out[name] * factor).astype(out[name].dtype)
    return out
```

```python
import concourse.bass as bass
from concourse import mybir
from contextlib import ExitStack
import numpy as np

F32 = mybir.dt.float32
BF16 = mybir.dt.bfloat16
ALU = mybir.AluOpType
ACT = mybir.ActivationFunctionType
AX = mybir.AxisListType

B, SIDE, C = 8, 32, 256
T = SIDE * SIDE
P = 128
NT = T // P
HALVES = C // P
ROWS = P // SIDE
NH = 8
HD = C // NH
BANK = 512
INNER = 512
DH = INNER // NH
IT = INNER // P
TAPS = 4
WIN = 7
NEG = -1.0e30
MASKW = (2 * (NT - 1) * ROWS + ROWS) * SIDE


class Layer:

    def __init__(self, nc, ctx, tag):
        self.nc, self.ctx, self.tag, self.sems = nc, ctx, tag, []
        self.ps = ctx.enter_context(nc.psum_tensor(tag + "_psum", [P, 8 * BANK], F32))

    def sb(self, name, shape, dt=F32):
        return self.ctx.enter_context(self.nc.sbuf_tensor(self.tag + "_" + name, shape, dt))

    def sem(self, name):
        s = self.ctx.enter_context(self.nc.semaphore(self.tag + "_" + name))
        self.sems.append(s)
        return s

    def barrier_and_clear(self):
        nums = sorted(s.num for s in self.sems)
        starts = [n for n in nums if n - 1 not in nums]
        ends = [n + 1 for n in nums if n + 1 not in nums]
        for first, end in zip(starts, ends):
            self.nc.all_engine_barrier(sems_to_clear=range(first, end))


class Chain:

    def __init__(self, sem):
        self.sem, self.n = sem, 0

    def restart(self):
        self.n = 0

    def __call__(self, eng, ins):
        self.n += 1
        ins.then_inc(self.sem, 1)
        eng.wait_ge(self.sem, self.n)


def shape_constants():
    f = np.float32
    c = {}
    tok = np.arange(T)
    part = np.arange(P)
    pr, pc = part // SIDE, part % SIDE
    half = 1.0 / 10000.0 ** np.linspace(0.0, 1.0, HD // 2)
    angle = np.repeat(half, 2).astype(f)
    index = (tok // SIDE + tok % SIDE).astype(f)
    ph = (np.tile(angle, P // HD)[:, None] * index[None, :]).astype(f)
    sign = np.where(part % 2 == 0, -1.0, 1.0)[:, None]
    c["rot_cos"] = np.cos(ph).astype(f)
    c["rot_sin"] = (np.sin(ph) * sign).astype(f)
    decay = np.log(1.0 - 2.0 ** (-2.0 - 5.0 * np.arange(NH) / NH))
    rel = np.arange(MASKW // SIDE) - (NT - 1) * ROWS
    col = np.arange(SIDE)
    d = np.abs(rel[None, :, None] - pr[:, None, None]) + np.abs(col[None, None, :] - pc[:, None, None])
    c["decay"] = np.exp(d[:, None] * decay[None, :, None, None]).reshape(P, NH * MASKW).astype(f)
    line = np.exp(np.abs(col[:, None] - col[None, :])[None] * decay[:, None, None]).sum(-1)
    rowsum = (line[:, :, None] * line[:, None, :]).reshape(NH, T)
    scale = np.repeat(HD ** -0.5 / np.sqrt(rowsum), HD, 0)
    c["row_scale"] = scale.reshape(HALVES, P, T).transpose(1, 0, 2).reshape(P, HALVES * T).astype(f)
    c["group_mean"] = np.kron(np.eye(P // 8), np.full((8, 8), 1.0 / 8.0)).astype(f)
    c["head_mean"] = np.kron(np.eye(P // HD), np.full((HD, HD), 1.0 / HD)).astype(f)
    c["ident"] = np.eye(P, dtype=f)
    c["causal"] = np.where(part[:, None] <= part[None, :], 0.0, NEG).astype(f)
    sel = np.zeros((NH, IT, P))
    for h in range(NH):
        sel[h, h // 2, (h % 2) * DH:(h % 2 + 1) * DH] = 1.0
    c["pair_sel"] = sel.reshape(NH, IT * P).astype(f)
    def window(tile, blocks):
        kt = np.arange(blocks[0] * P, blocks[1] * P)
        kr, kc = kt // SIDE, kt % SIDE
        qr = tile * ROWS + pr
        r0 = np.clip(qr - WIN // 2, 0, SIDE - WIN)
        c0 = np.clip(pc - WIN // 2, 0, SIDE - WIN)
        ok = (kr[None] >= r0[:, None]) & (kr[None] < r0[:, None] + WIN)
        ok &= (kc[None] >= c0[:, None]) & (kc[None] < c0[:, None] + WIN)
        return np.where(ok, 0.0, NEG)
    c["window"] = np.concatenate([window(0, (0, 2)), window(3, (2, 5)), window(NT - 1, (NT - 2, NT))], 1).astype(f)
    dist, out = [], []
    for tile, b0, b1 in ((0, 0, 2), (3, 2, 5), (NT - 1, NT - 2, NT)):
        kt = np.arange(b0 * P, b1 * P)
        dr = kt[None] // SIDE - (tile * ROWS + pr)[:, None]
        dc = kt[None] % SIDE - pc[:, None]
        ok = (np.abs(dr) <= WIN // 2) & (np.abs(dc) <= WIN // 2)
        npad = PADS[len(dist)]
        pd, po = np.zeros((P, npad)), np.full((P, npad), NEG)
        for q in range(P):
            n = 0
            for a in range(-(WIN // 2), WIN // 2 + 1):
                for e in range(-(WIN // 2), WIN // 2 + 1):
                    r, k = tile * ROWS + pr[q] + a, pc[q] + e
                    if not (0 <= r < SIDE and 0 <= k < SIDE):
                        pd[q, n], po[q, n] = np.sqrt(float(a * a + e * e)), 0.0
                        n += 1
        dist.append(np.concatenate([np.where(ok, np.sqrt(dr * dr + dc * dc), 0.0), pd], 1))
        out.append(np.concatenate([np.where(ok, 0.0, NEG), po], 1))
    c["dist"] = np.concatenate(dist, 1).astype(f)
    c["outside"] = np.concatenate(out, 1).astype(f)
    return c


_SIDE_PADS = (WIN // 2) * WIN
_CORNER_PADS = WIN * WIN - (WIN // 2 + 1) ** 2
PADS = (_CORNER_PADS, _SIDE_PADS, _CORNER_PADS)


RPB_ROWS = (1, 1)


def tile_class(t):
    return 0 if t == 0 else 2 if t == NT - 1 else 1


def key_blocks(t):
    return max(t - 1, 0), min(t + 2, NT)


def groupnorm(nc, L, g, x_in, xn, bank, b, load=None):
    with nc.Block() as block:
        if load is not None:
            @block.sync
            def _(sp):
                sp.dma_start(x_in[:, :, :], load[b, :, :, :]).then_inc(g.loaded, 16)

        @block.vector
        def _(dve):
            if load is not None:
                dve.wait_ge(g.loaded, 16)
            for hf in range(HALVES):
                for s in range(T // BANK):
                    i = nc.vector.bn_stats(g.stats[:, hf, s, :], x_in[:, hf, s * BANK:(s + 1) * BANK])
            g.v(dve, i)
            for hf in range(HALVES):
                i = nc.vector.bn_aggr(g.mv[:, hf, :], g.stats[:, hf, :, :].rearrange("p s k -> p (s k)"))
            g.v(dve, i)
            g.v(dve, nc.vector.tensor_tensor(g.sq[:, :], g.mv[:, :, 0], g.mv[:, :, 0], ALU.mult))
            nc.vector.tensor_tensor(g.mv[:, :, 1], g.mv[:, :, 1], g.sq[:, :], ALU.add).then_inc(g.chan, 1)
            dve.wait_ge(g.group, 1)
            g.v(dve, nc.vector.tensor_copy(g.gm[:, :], bank[:, 0:2 * HALVES]))
            gm = g.gm[:, :].rearrange("p (h k) -> p h k", k=2)
            g.v(dve, nc.vector.tensor_tensor(g.sq[:, :], gm[:, :, 0], gm[:, :, 0], ALU.mult))
            g.v(dve, nc.vector.tensor_tensor(g.sq[:, :], gm[:, :, 1], g.sq[:, :], ALU.subtract))
            nc.vector.tensor_scalar(g.sq[:, :], g.sq[:, :], 0.0, 1e-5, ALU.max, ALU.add).then_inc(g.var, 1)
            dve.wait_ge(g.sd, 1)
            g.v(dve, nc.vector.reciprocal(g.rstd[:, :], g.root[:, :]))
            g.v(dve, nc.vector.scalar_tensor_tensor(g.shift[:, :], gm[:, :, 0], -1.0, g.rstd[:, :],
                                                    ALU.mult, ALU.mult))
            for hf in range(HALVES):
                i = nc.vector.tensor_scalar(xn[:, hf, :], x_in[:, hf, :], g.rstd[:, hf:hf + 1],
                                            g.shift[:, hf:hf + 1], ALU.mult, ALU.add)
            g.v(dve, i)

        @block.tensor
        def _(pe):
            pe.wait_ge(g.chan, 1)
            nc.tensor.matmul(bank[:, 0:2 * HALVES], g.group_mean[:, :],
                             g.mv[:, :, :].rearrange("p h k -> p (h k)"), start=True, stop=True).then_inc(g.group, 1)

        @block.scalar
        def _(act):
            act.wait_ge(g.var, 1)
            nc.scalar.activation(g.root[:, :], g.sq[:, :], ACT.Sqrt).then_inc(g.sd, 1)


class Norm:

    def __init__(self, L, v):
        self.v = v
        self.stats = L.sb("gn_stats", [P, HALVES, T // BANK, 6])
        self.mv = L.sb("gn_mean_var", [P, HALVES, 2])
        self.gm = L.sb("gn_group", [P, 2 * HALVES])
        self.sq = L.sb("gn_sq", [P, HALVES])
        self.root = L.sb("gn_root", [P, HALVES])
        self.rstd = L.sb("gn_rstd", [P, HALVES])
        self.shift = L.sb("gn_shift", [P, HALVES])
        self.group_mean = L.sb("gn_group_mean", [P, P])
        self.loaded = L.sem("gn_loaded")
        self.chan = L.sem("gn_channel_stats")
        self.group = L.sem("gn_group_stats")
        self.var = L.sem("gn_variance")
        self.sd = L.sem("gn_deviation")


def load_all(nc, L, pairs):
    done = L.sem("weights")
    with nc.Block() as block:
        @block.sync
        def _(sp):
            for n, (dst, src) in enumerate(pairs):
                if n % 2 == 0:
                    sp.dma_start(dst, src).then_inc(done, 16)
            sp.wait_ge(done, 16 * len(pairs))

        @block.scalar
        def _(act):
            for n, (dst, src) in enumerate(pairs):
                if n % 2 == 1:
                    act.dma_start(dst, src).then_inc(done, 16)


class Split:
    Q = ((0, 1, 2), (0, 0, 1))
    K = ((0, 0, 0), (1, 2, 1))
    ROWS = 3 * HD
    SLOTS = 4

    def __init__(self, L, parts=None):
        self.parts = parts if parts is not None else [L.sb(f"part{s}", [P, 2 * HALVES, T], BF16) for s in range(3)]
        self.q = L.sb("q_stack", [self.ROWS, self.SLOTS, 2, T], BF16)
        self.k = L.sb("k_stack", [self.ROWS, self.SLOTS, 2, T], BF16)
        self.part_ready = L.sem("part_ready")
        self.rest_ready = L.sem("rest_ready")
        self.loaded = [L.sem(f"stack_loaded{s}") for s in range(self.SLOTS)]

    def scalar(self, nc, act, qk, ready=None):
        for g in range(HALVES):
            if ready is not None:
                act.wait_ge(ready, HALVES + g + 1)
            for part in range(3):
                for side in range(2):
                    u = side * HALVES + g
                    if part > 0:
                        act.wait_ge(self.rest_ready, 4 * g + 2 * (part - 1) + side + 1)
                    nc.scalar.activation(self.parts[part][:, u, :], qk[:, u, :], ACT.Copy).then_inc(self.part_ready, 1)

    def vector(self, nc, dve, qk, halves=range(HALVES)):
        for g in halves:
            for part in range(2):
                for side in range(2):
                    u = side * HALVES + g
                    dve.wait_ge(self.part_ready, 6 * g + 2 * part + side + 1)
                    if part > 0:
                        dve.wait_ge(self.rest_ready, 4 * g + 2 * (part - 1) + side + 1)
                    nc.vector.tensor_tensor(qk[:, u, :], qk[:, u, :], self.parts[part][:, u, :],
                                            ALU.subtract).then_inc(self.rest_ready, 1)

    def sync(self, nc, sp, scores_ready):
        for h in range(NH):
            sp.wait_ge(self.part_ready, 6 * (h // 4 + 1))
            if h >= self.SLOTS:
                sp.wait_ge(scores_ready, NT * (h - self.SLOTS + 1))
            r = (h % 4) * HD
            for side, stack, which in ((0, self.q, self.Q), (1, self.k, self.K)):
                for m in range(2):
                    for j, part in enumerate(which[m]):
                        sp.dma_start(stack[j * HD:(j + 1) * HD, h % self.SLOTS, m, :],
                                     self.parts[part][r:r + HD, side * HALVES + h // 4, :]
                                     ).then_inc(self.loaded[h % self.SLOTS], 16)

    def wait(self, pe, h):
        pe.wait_ge(self.loaded[h % self.SLOTS], 16 * 12 * (h // self.SLOTS + 1))


def project(nc, out, w, act, m, n0, n1):
    tiles = w.shape[1]
    for k in range(tiles):
        i = nc.tensor.matmul(out, w[:, k, m * P:(m + 1) * P], act[:, k, n0:n1], start=(k == 0), stop=(k == tiles - 1))
    return i


def project_tokens(nc, out, act, w, t):
    tiles = w.shape[1]
    for k in range(tiles):
        i = nc.tensor.matmul(out, act[:, k, t * P:(t + 1) * P], w[:, k, :], start=(k == 0), stop=(k == tiles - 1))
    return i


def layer0(nc, A, x, y):
    with ExitStack() as ctx:
        L = Layer(nc, ctx, "l0")
        vstep = Chain(L.sem("vstep"))
        g = Norm(L, vstep)
        PS = L.ps
        wq = L.sb("wq", [P, HALVES, C])
        wk = L.sb("wk", [P, HALVES, C])
        wv = L.sb("wv", [P, HALVES, C])
        wo = L.sb("wo", [P, HALVES, C])
        ident = L.sb("ident", [P, P])
        cos = L.sb("rot_cos", [P, T])
        sin = L.sb("rot_sin", [P, T])
        decay = L.sb("decay", [P, NH, MASKW])
        row_scale = L.sb("row_scale", [P, HALVES, T])
        head_mean = L.sb("head_mean", [P, P])
        ln_g = L.sb("ln_g", [P, 1])
        ln_b = L.sb("ln_b", [P, 1])
        ones = L.sb("ones", [P, HD])
        eps = L.sb("eps", [P, 1])
        xtok = L.sb("xtok", [P, NT, C])
        xT = L.sb("xT", [P, HALVES, T])
        xn = L.sb("xn", [P, HALVES, T])
        raw = L.sb("raw", [P, 2, T])
        swapped = L.sb("swapped", [P, 2, T])
        by_cos = L.sb("by_cos", [P, 2, T])
        qk = L.sb("qk", [P, 2 * HALVES, T])
        V = L.sb("V", [P, NT, C])
        probs = L.sb("probs", [P, 3, T])
        sizes, absv = swapped, by_cos
        square, rec, gT = swapped, by_cos, raw
        O, D = qk[:, 0:HALVES, :], qk[:, HALVES:2 * HALVES, :]
        parts = [t[:, :, :].rearrange("p a n -> p (a n)").bitcast(BF16).rearrange("p (u n) -> p u n", n=T)
                 for t in (xtok, xn, raw)]
        split = Split(L, parts)

        x_loaded, x_turned, x_copied = L.sem("x_loaded"), L.sem("x_turned"), L.sem("x_copied")
        proj_done, raw_ready, sw_ready = L.sem("proj_done"), L.sem("raw_ready"), L.sem("sw_ready")
        sin_ready, rot_done = L.sem("sin_ready"), L.sem("rot_done")
        v_done, v_copied = L.sem("v_done"), L.sem("v_copied")
        scores_ready, probs_ready = L.sem("scores_ready"), L.sem("probs_ready")
        abs_ready, size_added = L.sem("abs_ready"), L.sem("size_added")
        unit_used, head_done, head_copied = L.sem("unit_used"), L.sem("head_done"), L.sem("head_copied")
        o_ready, mean_ready, centred, squared = L.sem("o_ready"), L.sem("mean_ready"), L.sem("centred"), L.sem("squared")
        var_ready, dev_ready, y_ready, g_ready = L.sem("var_ready"), L.sem("dev_ready"), L.sem("y_ready"), L.sem("g_ready")
        den_ready, log_ready, inv_ready = L.sem("den_ready"), L.sem("log_ready"), L.sem("inv_ready")
        out_done, added, stored = L.sem("out_done"), L.sem("added"), L.sem("stored")

        def wview(w):
            return w.rearrange("(k p) n -> p k n", p=P)

        load_all(nc, L, [
            (wq[:, :, :], wview(A["L0_WqT"])), (wk[:, :, :], wview(A["L0_WkT"])),
            (wv[:, :, :], wview(A["L0_WvT"])), (wo[:, :, :], wview(A["L0_WoT"])),
            (ident[:, :], A["ident"]), (g.group_mean[:, :], A["group_mean"]),
            (cos[:, :], A["rot_cos"]), (sin[:, :], A["rot_sin"]),
            (decay[:, 0:4, :].rearrange("p h n -> p (h n)"), A["decay"][:, 0:4 * MASKW]),
            (decay[:, 4:8, :].rearrange("p h n -> p (h n)"), A["decay"][:, 4 * MASKW:8 * MASKW]),
            (row_scale[:, :, :].rearrange("p h n -> p (h n)"), A["row_scale"]),
            (head_mean[:, :], A["head_mean"]), (ln_g[:, :], A["L0_ln_g"]), (ln_b[:, :], A["L0_ln_b"]),
        ])
        with nc.Block() as block:
            @block.vector
            def _(dve):
                nc.vector.memset(eps[:, :], 1e-5)
                vstep(dve, nc.vector.memset(ones[:, :], 1.0))
        L.barrier_and_clear()
        vstep.restart()

        with nc.Fori(0, B) as b:
            with nc.Block() as block:
                @block.sync
                def _(sp):
                    for t2 in range(2):
                        src = x[b, t2 * SIDE // 2:(t2 + 1) * SIDE // 2, :, :].rearrange("(t r) w c -> (r w) t c", r=ROWS)
                        sp.dma_start(xtok[:, t2 * 4:t2 * 4 + 4, :], src).then_inc(x_loaded, 16)

                @block.tensor
                def _(pe):
                    pe.wait_ge(x_loaded, 32)
                    for hf in range(HALVES):
                        for t in range(NT):
                            i = nc.tensor.transpose(PS[:, hf * T + t * P:hf * T + (t + 1) * P],
                                                    xtok[:, t, hf * P:(hf + 1) * P], ident[:, :])
                            if t % 4 == 3:
                                i.then_inc(x_turned, 1)

                @block.vector
                def _(dve):
                    for k in (0, 2):
                        dve.wait_ge(x_turned, k + 1)
                        i = nc.vector.tensor_copy(xT[:, k // 2, (k % 2) * BANK:(k % 2 + 1) * BANK],
                                                  PS[:, k * BANK:(k + 1) * BANK])
                    i.then_inc(x_copied, 1)

                @block.scalar
                def _(act):
                    for k in (1, 3):
                        act.wait_ge(x_turned, k + 1)
                        i = nc.scalar.activation(xT[:, k // 2, (k % 2) * BANK:(k % 2 + 1) * BANK],
                                                 PS[:, k * BANK:(k + 1) * BANK], ACT.Copy)
                    i.then_inc(x_copied, 1)

            groupnorm(nc, L, g, xT, xn, PS, b)

            with nc.Block() as block:
                @block.tensor
                def _(pe):
                    for u in range(2 * HALVES):
                        w = wq if u < HALVES else wk
                        for n in range(2):
                            i = project(nc, PS[:, u * T + n * BANK:u * T + (n + 1) * BANK], w, xn, u % 2,
                                        n * BANK, (n + 1) * BANK)
                        i.then_inc(proj_done, 1)
                    for t in range(NT):
                        if t == 0:
                            pe.wait_ge(raw_ready, 2)
                        i = project_tokens(nc, PS[:, t * C:(t + 1) * C], xn, wv, t)
                        if t % 2 == 1:
                            i.then_inc(v_done, 1)

                @block.scalar
                def _(act):
                    for u in range(2 * HALVES):
                        act.wait_ge(proj_done, u + 1)
                        if u >= 2:
                            act.wait_ge(rot_done, u - 1)
                        nc.scalar.activation(raw[:, u % 2, :], PS[:, u * T:(u + 1) * T], ACT.Copy).then_inc(raw_ready, 1)
                    for k in range(NT // 2):
                        act.wait_ge(v_done, k + 1)
                        nc.scalar.activation(V[:, 2 * k:2 * k + 2, :].rearrange("p t c -> p (t c)"),
                                             PS[:, k * BANK:(k + 1) * BANK], ACT.Copy).then_inc(v_copied, 1)

                @block.vector
                def _(dve):
                    def combine(u):
                        dve.wait_ge(sin_ready, u + 1)
                        nc.vector.tensor_tensor(qk[:, u, :], by_cos[:, u % 2, :], swapped[:, u % 2, :],
                                                ALU.add).then_inc(rot_done, 1)

                    for u in range(2 * HALVES):
                        if u >= 2:
                            combine(u - 2)
                            dve.wait_ge(rot_done, u - 1)
                        dve.wait_ge(raw_ready, u + 1)
                        nc.vector.stream_shuffle(swapped[:, u % 2, :], raw[:, u % 2, :],
                                                 [p ^ 1 for p in range(32)]).then_inc(sw_ready, 1)
                        vstep(dve, nc.vector.tensor_tensor(by_cos[:, u % 2, :], raw[:, u % 2, :], cos[:, :], ALU.mult))
                    combine(2)
                    combine(3)

                @block.gpsimd
                def _(pool):
                    for u in range(2 * HALVES):
                        pool.wait_ge(sw_ready, u + 1)
                        nc.gpsimd.tensor_tensor(swapped[:, u % 2, :], swapped[:, u % 2, :], sin[:, :],
                                                ALU.mult).then_inc(sin_ready, 1)

            with nc.Block() as block:
                UNITS = NH * NT
                LAG = 1

                def size_adds(n):
                    return n // NT * (NT - 1) + max(n % NT - 1, 0)

                @block.sync
                def _(sp):
                    split.sync(nc, sp, scores_ready)

                @block.tensor
                def _(pe):
                    def weigh(n):
                        h, J = n // NT, n % NT
                        r = (h % 4) * HD
                        pe.wait_ge(probs_ready, n + 1)
                        if J == 0 and h >= 4:
                            pe.wait_ge(head_copied, h - 3)
                        for m in range(2):
                            i = nc.tensor.matmul(PS[r:r + HD, (4 + m) * BANK:(5 + m) * BANK],
                                                 V[:, J, h * HD:(h + 1) * HD],
                                                 probs[:, n % 3, m * BANK:(m + 1) * BANK],
                                                 start=(J == 0), stop=(J == NT - 1))
                        i.then_inc(unit_used, 1)
                        if J == NT - 1:
                            pe.wait_ge(size_added, size_adds(n + 1))
                            for m in range(2):
                                i = nc.tensor.matmul(PS[r:r + HD, (6 + m) * BANK:(7 + m) * BANK], ones[:, :],
                                                     sizes[:, h % 2, m * BANK:(m + 1) * BANK], start=True, stop=True)
                            i.then_inc(head_done, 1)

                    for n in range(UNITS + LAG):
                        if n < UNITS:
                            h, J = n // NT, n % NT
                            if n >= 2:
                                pe.wait_ge(probs_ready, n - 1)
                            if J == 0:
                                split.wait(pe, h)
                            slot = h % split.SLOTS
                            for m in range(2):
                                c0 = (n % 2) * T + m * BANK
                                for e in range(2):
                                    i = nc.tensor.matmul(PS[:, c0:c0 + BANK], split.k[:, slot, e, J * P:(J + 1) * P],
                                                         split.q[:, slot, e, m * BANK:(m + 1) * BANK],
                                                         start=(e == 0), stop=(e == 1))
                            i.then_inc(scores_ready, 1)
                        if n >= LAG:
                            weigh(n - LAG)

                @block.vector
                def _(dve):
                    split.vector(nc, dve, qk)
                    for n in range(UNITS):
                        h, J = n // NT, n % NT
                        dve.wait_ge(scores_ready, n + 1)
                        if n >= 3:
                            dve.wait_ge(unit_used, n - 2)
                            dve.wait_ge(abs_ready, n - 2)
                        s0 = (NT - 1 - J) * ROWS * SIDE
                        nc.vector.tensor_tensor(probs[:, n % 3, :], PS[:, (n % 2) * T:(n % 2 + 1) * T],
                                                decay[:, h, s0:s0 + T], ALU.mult).then_inc(probs_ready, 1)

                @block.scalar
                def _(act):
                    def copy_head(h):
                        r = (h % 4) * HD
                        act.wait_ge(head_done, h + 1)
                        nc.scalar.activation(O[r:r + HD, h // 4, :], PS[r:r + HD, 4 * BANK:6 * BANK], ACT.Copy)
                        nc.scalar.activation(D[r:r + HD, h // 4, :], PS[r:r + HD, 6 * BANK:8 * BANK],
                                             ACT.Copy).then_inc(head_copied, 1)

                    split.scalar(nc, act, qk)
                    for n in range(UNITS):
                        h, J = n // NT, n % NT
                        act.wait_ge(probs_ready, n + 1)
                        if J == 0:
                            if h >= 2:
                                act.wait_ge(head_done, h - 1)
                            nc.scalar.activation(sizes[:, h % 2, :], probs[:, n % 3, :], ACT.Abs).then_inc(abs_ready, 1)
                        else:
                            if n >= 3:
                                act.wait_ge(size_added, size_adds(n - 1))
                            nc.scalar.activation(absv[:, n % 2, :], probs[:, n % 3, :], ACT.Abs).then_inc(abs_ready, 1)
                        if J == 2 and h >= 1:
                            copy_head(h - 1)
                    copy_head(NH - 1)

                @block.gpsimd
                def _(pool):
                    for n in range(UNITS):
                        h, J = n // NT, n % NT
                        pool.wait_ge(abs_ready, n + 1)
                        if J >= 1:
                            if J >= 2:
                                pool.wait_ge(size_added, size_adds(n))
                            size = sizes[:, h % 2, :]
                            nc.gpsimd.tensor_tensor(size, size, absv[:, n % 2, :], ALU.add).then_inc(size_added, 1)

            with nc.Block() as block:
                @block.vector
                def _(dve):
                    for hf in range(HALVES):
                        vstep(dve, nc.vector.tensor_tensor(D[:, hf, :], D[:, hf, :], row_scale[:, hf, :], ALU.mult))
                        nc.vector.tensor_scalar(D[:, hf, :], D[:, hf, :], 1.0, 50000.0, ALU.max,
                                                ALU.min).then_inc(den_ready, 1)
                    for hf in range(HALVES):
                        vstep(dve, nc.vector.tensor_tensor(O[:, hf, :], O[:, hf, :], row_scale[:, hf, :], ALU.mult))
                        dve.wait_ge(inv_ready, hf + 1)
                        nc.vector.tensor_tensor(O[:, hf, :], O[:, hf, :], rec[:, hf, :], ALU.mult).then_inc(o_ready, 1)
                    for hf in range(HALVES):
                        dve.wait_ge(mean_ready, hf + 1)
                        nc.vector.tensor_tensor(O[:, hf, :], O[:, hf, :], PS[:, hf * T:(hf + 1) * T],
                                                ALU.subtract).then_inc(centred, 1)
                    for hf in range(HALVES):
                        dve.wait_ge(dev_ready, hf + 1)
                        nc.vector.tensor_tensor(O[:, hf, :], O[:, hf, :], rec[:, hf, :], ALU.mult).then_inc(y_ready, 1)
                    for k in range(2 * HALVES):
                        dve.wait_ge(out_done, k + 1)
                        s = slice((k % 2) * BANK, (k % 2 + 1) * BANK)
                        nc.vector.tensor_tensor(xT[:, k // 2, s], xT[:, k // 2, s], PS[:, k * BANK:(k + 1) * BANK],
                                                ALU.add).then_inc(added, 1)

                @block.scalar
                def _(act):
                    for hf in range(HALVES):
                        act.wait_ge(den_ready, hf + 1)
                        nc.scalar.activation(rec[:, hf, :], D[:, hf, :], ACT.Ln).then_inc(log_ready, 1)
                    for hf in range(HALVES):
                        act.wait_ge(log_ready, hf + 1)
                        nc.scalar.activation(rec[:, hf, :], rec[:, hf, :], ACT.Exp, scale=-1.0).then_inc(inv_ready, 1)
                    for hf in range(HALVES):
                        act.wait_ge(centred, hf + 1)
                        nc.scalar.activation(square[:, hf, :], O[:, hf, :], ACT.Square).then_inc(squared, 1)
                    for hf in range(HALVES):
                        act.wait_ge(var_ready, hf + 1)
                        nc.scalar.activation(rec[:, hf, :], PS[:, (2 + hf) * T:(3 + hf) * T], ACT.Ln,
                                             bias=eps[:, :]).then_inc(log_ready, 1)
                    for hf in range(HALVES):
                        act.wait_ge(log_ready, HALVES + hf + 1)
                        nc.scalar.activation(rec[:, hf, :], rec[:, hf, :], ACT.Exp, scale=-0.5).then_inc(dev_ready, 1)
                    for hf in range(HALVES):
                        act.wait_ge(y_ready, hf + 1)
                        nc.scalar.activation(gT[:, hf, :], O[:, hf, :], ACT.Gelu, bias=ln_b[:, :],
                                             scale=ln_g[:, :]).then_inc(g_ready, 1)

                @block.tensor
                def _(pe):
                    def head_means(bank, src):
                        for m in range(2):
                            i = nc.tensor.matmul(PS[:, (bank + m) * BANK:(bank + m + 1) * BANK], head_mean[:, :],
                                                 src[:, m * BANK:(m + 1) * BANK], start=True, stop=True)
                        return i

                    for hf in range(HALVES):
                        pe.wait_ge(o_ready, hf + 1)
                        head_means(2 * hf, O[:, hf, :]).then_inc(mean_ready, 1)
                    for hf in range(HALVES):
                        pe.wait_ge(squared, hf + 1)
                        head_means(4 + 2 * hf, square[:, hf, :]).then_inc(var_ready, 1)
                    pe.wait_ge(g_ready, HALVES)
                    for k in range(2 * HALVES):
                        m, n = k // 2, k % 2
                        project(nc, PS[:, k * BANK:(k + 1) * BANK], wo, gT, m, n * BANK,
                                (n + 1) * BANK).then_inc(out_done, 1)

                @block.sync
                def _(sp):
                    sp.wait_ge(added, 2 * HALVES)
                    sp.dma_start(y[b, :, :, :], xT[:, :, :]).then_inc(stored, 16)
                    sp.wait_ge(stored, 16)
            L.barrier_and_clear()
            vstep.restart()


def layer1(nc, A, x, y, scratch):
    with ExitStack() as ctx:
        L = Layer(nc, ctx, "l1")
        vstep, astep = Chain(L.sem("vstep")), Chain(L.sem("astep"))
        g = Norm(L, vstep)
        PS = L.ps
        D1 = DH + 1
        FG = 32
        wup = L.sb("w_up", [P, HALVES, 2 * INNER])
        wbd = L.sb("w_qkv", [P, 3, IT, P])
        wdn = L.sb("w_down", [P, IT, C])
        ident = L.sb("ident", [P, P])
        causal = L.sb("causal", [P, P])
        pair_sel = L.sb("pair_sel", [NH, IT, P])
        conv_w = L.sb("conv_w", [P, IT, TAPS])
        cols = L.sb("cols", [P, 3, IT])
        gate_b = L.sb("gate_b", [P, 1])
        wg = L.sb("w_gate", [P, 2 * IT, FG + NH])
        xT = L.sb("xT", [P, HALVES, T])
        xn = L.sb("xn", [P, HALVES, T])
        xm = L.sb("xm", [P, IT, T + TAPS - 1])
        sz = L.sb("silu_z", [P, IT, T])
        xa = L.sb("x_act", [P, IT, T])
        qT = L.sb("qT", [P, IT, T])
        kT = L.sb("kT", [P, IT, T])
        vT = L.sb("vT", [P, IT, T])
        kt = L.sb("k_tok", [P, NT, INNER])
        v1 = L.sb("v_tok", [P, NT, NH, D1])
        rows = L.sb("rows", [NH, 4, T])
        tokv = L.sb("tok_vals", [P, 3, NT, NH])
        chunk_max = L.sb("chunk_max", [NH, 3, NT])
        fade = L.sb("fade", [P, IT, NT])
        cmb = L.sb("c_everywhere", [P, 2, NH, P])
        E = L.sb("E", [P, 2, NH, P])
        state = L.sb("state", [P, IT, D1])
        den = L.sb("den", [P, NH])
        nrm = L.sb("nrm", [P, NH])
        mu = L.sb("mu", [P, NH])
        var = L.sb("var", [P, NT, NH])
        rstd = L.sb("rstd", [P, NT, NH])
        sq = L.sb("sq", [P, NH, DH])
        conv = kt[:, :, :].rearrange("p t c -> p (t c)").rearrange("p (i n) -> p i n", i=IT)
        H = vT[:, :, :].rearrange("p i n -> p (i n)").rearrange("p (t h d) -> p t h d", t=NT, h=NH)
        qw = xm[:, :, TAPS - 1:]
        Pr = xn[:, :, :].rearrange("p k (h n) -> p k h n", h=NH)
        hT = kT
        a_row, c_row, nc_row, lc_row = rows[:, 0, :], rows[:, 1, :], rows[:, 2, :], rows[:, 3, :]
        f_row, e_row = xn[0:NH, 0, :], xn[0:NH, 1, :]

        up_done, up_copied, conv_done, act_done = L.sem("up_done"), L.sem("up_copied"), L.sem("conv_done"), L.sem("act_done")
        qkv_done, qkv_copied, kv_turned, tok_copied = L.sem("qkv_done"), L.sem("qkv_copied"), L.sem("kv_turned"), L.sem("tok_copied")
        gates_done, f_ready, ln_ready, c_ready = L.sem("gates_done"), L.sem("f_ready"), L.sem("ln_ready"), L.sem("c_ready")
        rows_ready, vals_turned, vals_copied, c_stored = L.sem("rows_ready"), L.sem("vals_turned"), L.sem("vals_copied"), L.sem("c_stored")
        w_spread, qw_ready = L.sem("w_spread"), L.sem("qw_ready")
        cmb_loaded = [L.sem("cmb_loaded0"), L.sem("cmb_loaded1")]
        arg_ready, e_ready, s_ready, p_ready = L.sem("arg_ready"), L.sem("e_ready"), L.sem("s_ready"), L.sem("p_ready")
        kg_ready, av_done, u_done, state_ready = L.sem("kg_ready"), L.sem("av_done"), L.sem("u_done"), L.sem("state_ready")
        o_used, h_ready, sq_ready = L.sem("o_used"), L.sem("h_ready"), L.sem("sq_ready")
        sd_ready, skip_ready, h_scaled, h_turned = L.sem("sd_ready"), L.sem("skip_ready"), L.sem("h_scaled"), L.sem("h_turned")
        h_done, out_done, added, stored = L.sem("h_done"), L.sem("out_done"), L.sem("added"), L.sem("stored")
        folded = L.sem("folded")

        def ktiles(w, k):
            return w.rearrange("(k p) n -> p k n", k=k)

        load_all(nc, L, [
            (wup[:, :, :], ktiles(A["L1_WupT"], HALVES)), (wdn[:, :, :], ktiles(A["L1_WdownT"], IT)),
            (wbd[:, :, :, :].rearrange("p s i n -> p (s i n)"), A["L1_qkv"]),
            (qT[:, :, :].rearrange("p i n -> p (i n)")[:, 0:3 * IT * P], A["L1_qkvT"]),
            (kT[:, 0, 0:3 * IT * (FG + NH)], A["L1_gate_w"]),
            (ident[:, :], A["ident"]), (causal[:, :], A["causal"]), (g.group_mean[:, :], A["group_mean"]),
            (pair_sel[:, :, :].rearrange("p i n -> p (i n)"), A["pair_sel"]),
            (conv_w[:, :, :].rearrange("p i n -> p (i n)"), A["L1_conv_w"]),
            (cols[:, :, :].rearrange("p i n -> p (i n)"), A["L1_cols"]),
            (gate_b[0:NH, :], A["L1_b_i"]), (gate_b[FG:FG + NH, :], A["L1_b_f"]),
        ])
        with nc.Block() as block:
            back = qT[:, :, :].rearrange("p i n -> p (i n)")[:, 0:3 * IT * P].rearrange("p (s i n) -> p s i n", s=3, i=IT)
            gw = kT[:, 0, 0:3 * IT * (FG + NH)].rearrange("p (s i n) -> p s i n", s=3, i=IT)
            G = FG + NH

            @block.tensor
            def _(pe):
                for i in range(IT):
                    nc.tensor.matmul(PS[:, i * G:(i + 1) * G], back[:, 0, i, :], gw[:, 0, i, :], start=True, stop=False)
                    nc.tensor.matmul(PS[:, i * G:(i + 1) * G], back[:, 1, i, :], gw[:, 1, i, :], start=False, stop=True)
                for i in range(IT):
                    m = nc.tensor.matmul(PS[:, (IT + i) * G:(IT + i + 1) * G], back[:, 2, i, :], gw[:, 2, i, :],
                                         start=True, stop=True)
                m.then_inc(folded, 1)

            @block.vector
            def _(dve):
                dve.wait_ge(folded, 1)
                nc.vector.tensor_copy(wg[:, :, :].rearrange("p i n -> p (i n)"), PS[:, 0:2 * IT * G])
                nc.vector.memset(xm[:, :, 0:TAPS - 1], 0.0)
                vstep(dve, nc.vector.memset(v1[:, :, :, DH:D1], 1.0))
        L.barrier_and_clear()
        vstep.restart()

        with nc.Fori(0, B) as b:
            groupnorm(nc, L, g, xT, xn, PS, b, load=x)

            with nc.Block() as block:
                @block.tensor
                def _(pe):
                    for m in range(2 * IT):
                        if m >= 4:
                            pe.wait_ge(up_copied, m - 3)
                        for n in range(2):
                            i = project(nc, PS[:, (m % 4) * T + n * BANK:(m % 4) * T + (n + 1) * BANK], wup, xn, m,
                                        n * BANK, (n + 1) * BANK)
                        i.then_inc(up_done, 1)

                @block.scalar
                def _(act):
                    for m in range(2 * IT):
                        act.wait_ge(up_done, m + 1)
                        src = PS[:, (m % 4) * T:(m % 4 + 1) * T]
                        if m < IT:
                            nc.scalar.activation(xm[:, m, TAPS - 1:], src, ACT.Copy).then_inc(up_copied, 1)
                        else:
                            nc.scalar.activation(sz[:, m - IT, :], src, ACT.Silu).then_inc(up_copied, 1)
                    for m in range(IT):
                        act.wait_ge(conv_done, m + 1)
                        nc.scalar.activation(xa[:, m, :], conv[:, m, :], ACT.Silu).then_inc(act_done, 1)

                @block.vector
                def _(dve):
                    for m in range(IT):
                        dve.wait_ge(up_copied, m + 1)
                        vstep(dve, nc.vector.tensor_scalar(conv[:, m, :], xm[:, m, 0:T], conv_w[:, m, 0:1],
                                                           cols[:, 0, m:m + 1], ALU.mult, ALU.add))
                        for k in range(1, TAPS):
                            i = nc.vector.scalar_tensor_tensor(conv[:, m, :], xm[:, m, k:k + T], conv_w[:, m, k:k + 1],
                                                               conv[:, m, :], ALU.mult, ALU.add)
                            if k < TAPS - 1:
                                vstep(dve, i)
                        i.then_inc(conv_done, 1)

            with nc.Block() as block:
                GB = 6 * BANK

                @block.tensor
                def _(pe):
                    for n in range(2):
                        for i in range(2 * IT):
                            src = xa[:, i, n * BANK:(n + 1) * BANK] if i < IT else \
                                xm[:, i - IT, TAPS - 1 + n * BANK:TAPS - 1 + (n + 1) * BANK]
                            m = nc.tensor.matmul(PS[0:FG + NH, GB + n * BANK:GB + (n + 1) * BANK], wg[:, i, :], src,
                                                 start=(i == 0), stop=(i == 2 * IT - 1))
                    m.then_inc(gates_done, 1)
                    for j in range(3 * IT):
                        s, i = (1, 2, 0)[j // IT], j % IT
                        if j >= 3:
                            pe.wait_ge(qkv_copied, j - 2)
                        for n in range(2):
                            src = xm[:, i, TAPS - 1 + n * BANK:TAPS - 1 + (n + 1) * BANK] if s == 2 else \
                                xa[:, i, n * BANK:(n + 1) * BANK]
                            m = nc.tensor.matmul(PS[:, (j % 3) * T + n * BANK:(j % 3) * T + (n + 1) * BANK],
                                                 wbd[:, s, i, :], src, start=True, stop=True)
                        m.then_inc(qkv_done, 1)
                    pe.wait_ge(qkv_copied, 3 * IT)
                    for j in range(2 * NT):
                        src = kT if j < NT else vT
                        if j >= 6:
                            pe.wait_ge(tok_copied, j - 5)
                        for i in range(IT):
                            m = nc.tensor.transpose(PS[:, (j % 6) * BANK + i * P:(j % 6) * BANK + (i + 1) * P],
                                                    src[:, i, (j % NT) * P:(j % NT + 1) * P], ident[:, :])
                        m.then_inc(kv_turned, 1)
                    pe.wait_ge(rows_ready, 1)
                    for s, row in enumerate((a_row, f_row, lc_row)):
                        for t in range(NT):
                            c0 = GB + (s * NT + t) * NH
                            m = nc.tensor.transpose(PS[:, c0:c0 + NH], row[:, t * P:(t + 1) * P], ident[0:NH, 0:NH])
                    for i in range(IT):
                        c0 = GB + BANK + i * NT
                        m = nc.tensor.matmul(PS[:, c0:c0 + NT], pair_sel[:, i, :], chunk_max[:, 2, :], start=True, stop=True)
                    m.then_inc(vals_turned, 1)
                    pe.wait_ge(tok_copied, 2 * NT)
                    for i in range(IT):
                        if i >= 3:
                            pe.wait_ge(qw_ready, i - 2)
                        for n in range(2):
                            m = nc.tensor.matmul(PS[:, (i % 3) * T + n * BANK:(i % 3) * T + (n + 1) * BANK],
                                                 pair_sel[:, i, :], e_row[:, n * BANK:(n + 1) * BANK], start=True, stop=True)
                        m.then_inc(w_spread, 1)

                @block.scalar
                def _(act):
                    def copy_qkv(j):
                        act.wait_ge(qkv_done, j + 1)
                        src = PS[:, (j % 3) * T:(j % 3 + 1) * T]
                        i = j % IT
                        if j < IT:
                            m = nc.scalar.activation(kT[:, i, :], src, ACT.Copy, scale=DH ** -0.5)
                        elif j < 2 * IT:
                            m = nc.scalar.activation(vT[:, i, :], src, ACT.Copy)
                        else:
                            m = nc.scalar.activation(qT[:, i, :], src, ACT.Copy)
                        m.then_inc(qkv_copied, 1)

                    copy_qkv(0)
                    copy_qkv(1)
                    act.wait_ge(f_ready, 1)
                    astep(act, nc.scalar.activation(e_row, f_row, ACT.Abs))
                    astep(act, nc.scalar.activation(e_row, e_row, ACT.Exp, scale=-1.0))
                    nc.scalar.activation(e_row, e_row, ACT.Ln, bias=1.0).then_inc(ln_ready, 1)
                    for j in range(2, 3 * IT):
                        copy_qkv(j)
                    act.wait_ge(c_ready, 1)
                    for t in range(NT):
                        s = slice(t * P, (t + 1) * P)
                        if t >= 1:
                            nc.scalar.activation(e_row[:, s], c_row[:, s], ACT.Exp, scale=-1.0,
                                                 bias=chunk_max[:, 0, t - 1:t])
                        nc.scalar.activation(f_row[:, s], a_row[:, s], ACT.Exp, bias=chunk_max[:, 1, t:t + 1])
                    nc.scalar.activation(e_row[:, 0:P], c_row[:, 0:P], ACT.Exp, scale=0.0)
                    nc.scalar.activation(chunk_max[:, 2, :], chunk_max[:, 2, :], ACT.Exp)
                    nc.scalar.activation(lc_row, lc_row, ACT.Exp, scale=-1.0).then_inc(rows_ready, 1)
                    for j in range(0, 2 * NT, 2):
                        act.wait_ge(kv_turned, j + 1)
                        src = PS[:, (j % 6) * BANK:(j % 6 + 1) * BANK]
                        act.wait_ge(tok_copied, j)
                        if j < NT:
                            nc.scalar.activation(kt[:, j, :], src, ACT.Copy).then_inc(tok_copied, 1)
                        else:
                            nc.scalar.activation(v1[:, j - NT, :, 0:DH], src.rearrange("p (h d) -> p h d", d=DH),
                                                 ACT.Copy).then_inc(tok_copied, 1)

                @block.vector
                def _(dve):
                    dve.wait_ge(gates_done, 1)
                    gf = E[FG:FG + NH, :, :, :].rearrange("p a h n -> p (a h n)")[:, 0:T]
                    vstep(dve, nc.vector.tensor_scalar(gf, PS[FG:FG + NH, GB:GB + T], gate_b[FG:FG + NH, :], None, ALU.add))
                    nc.vector.tensor_copy(f_row, gf).then_inc(f_ready, 1)
                    vstep(dve, nc.vector.memset(a_row, 1.0))
                    dve.wait_ge(ln_ready, 1)
                    vstep(dve, nc.vector.scalar_tensor_tensor(f_row, f_row, 0.0, e_row, ALU.min, ALU.subtract))
                    vstep(dve, nc.vector.tensor_tensor_scan(lc_row, a_row, f_row, 0.0, ALU.mult, ALU.add))
                    vstep(dve, nc.vector.scalar_tensor_tensor(a_row, PS[0:NH, GB:GB + T], gate_b[0:NH, :], lc_row,
                                                              ALU.add, ALU.subtract))
                    vstep(dve, nc.vector.tensor_tensor_scan(c_row, a_row, a_row, -3.0e38, ALU.max, ALU.max))
                    ends = c_row.rearrange("p (t n) -> p t n", n=P)[:, :, P - 1]
                    nc.vector.tensor_scalar(nc_row, c_row, -1.0, None, ALU.mult)
                    nc.vector.tensor_copy(chunk_max[:, 0, :], ends)
                    nc.vector.tensor_scalar(chunk_max[:, 1, :], ends, -1.0, None, ALU.mult)
                    nc.vector.memset(chunk_max[:, 2, 0:1], 0.0)
                    vstep(dve, nc.vector.tensor_tensor(lc_row, lc_row, c_row, ALU.add))
                    nc.vector.tensor_tensor(chunk_max[:, 2, 1:NT], chunk_max[:, 0, 0:NT - 1], chunk_max[:, 0, 1:NT],
                                            ALU.subtract).then_inc(c_ready, 1)
                    for j in range(1, 2 * NT, 2):
                        dve.wait_ge(kv_turned, j + 1)
                        dve.wait_ge(tok_copied, j)
                        src = PS[:, (j % 6) * BANK:(j % 6 + 1) * BANK]
                        if j < NT:
                            nc.vector.tensor_copy(kt[:, j, :], src).then_inc(tok_copied, 1)
                        else:
                            nc.vector.tensor_copy(v1[:, j - NT, :, 0:DH],
                                                  src.rearrange("p (h d) -> p h d", d=DH)).then_inc(tok_copied, 1)
                    dve.wait_ge(vals_turned, 1)
                    nc.vector.tensor_copy(tokv[:, :, :, :].rearrange("p s t h -> p (s t h)"), PS[:, GB:GB + 3 * NT * NH])
                    nc.vector.tensor_copy(fade[:, :, :].rearrange("p i t -> p (i t)"),
                                          PS[:, GB + BANK:GB + BANK + IT * NT]).then_inc(vals_copied, 1)
                    for i in range(IT):
                        dve.wait_ge(w_spread, i + 1)
                        nc.vector.tensor_tensor(qw[:, i, :], PS[:, (i % 3) * T:(i % 3 + 1) * T], qT[:, i, :],
                                                ALU.mult).then_inc(qw_ready, 1)

                @block.sync
                def _(sp):
                    sp.wait_ge(c_ready, 1)
                    sp.dma_start(scratch, nc_row).then_inc(c_stored, 16)
                    sp.wait_ge(c_stored, 16)
                    for t in range(2):
                        sp.dma_start(cmb[:, t, :, :], scratch[:, t * P:(t + 1) * P].partition_broadcast(P)
                                     ).then_inc(cmb_loaded[t], 16)

            with nc.Block() as block:
                def o_all():
                    return PS[:, 4 * BANK:6 * BANK].rearrange("p (b a c) -> p a b c", b=2, c=P)

                def by_pair(ap):
                    return ap.rearrange("p (a b) n -> p a b n", b=2)

                @block.sync
                def _(sp):
                    for t in range(2, NT):
                        sp.wait_ge(arg_ready, t - 1)
                        sp.dma_start(cmb[:, t % 2, :, :], scratch[:, t * P:(t + 1) * P].partition_broadcast(P)
                                     ).then_inc(cmb_loaded[t % 2], 16)

                @block.tensor
                def _(pe):
                    def scores(t):
                        if t >= 2:
                            pe.wait_ge(p_ready, t - 1)
                        for h in range(NH):
                            r = (h % 2) * DH
                            c0 = (t % 2) * T + (h % 2) * BANK + h // 2 * P
                            i = nc.tensor.matmul(PS[:, c0:c0 + P],
                                                 kT[r:r + DH, h // 2, t * P:(t + 1) * P],
                                                 qT[r:r + DH, h // 2, t * P:(t + 1) * P], start=True, stop=True)
                        i.then_inc(s_ready, 1)

                    scores(0)
                    for t in range(NT):
                        if t + 1 < NT:
                            scores(t + 1)
                        pe.wait_ge(p_ready, t + 1)
                        if t >= 1:
                            pe.wait_ge(o_used, t)
                            pe.wait_ge(state_ready, t)
                        o = o_all()
                        for h in range(NH):
                            r = (h % 2) * DH
                            i = nc.tensor.matmul(o[:, h // 2, h % 2, 0:D1], Pr[:, t % 2, h, :], v1[:, t, h, :], start=True, stop=(t == 0))
                            if t >= 1:
                                i = nc.tensor.matmul(o[:, h // 2, h % 2, 0:D1], qw[r:r + DH, h // 2, t * P:(t + 1) * P],
                                                     state[r:r + DH, h // 2, :], start=False, stop=True)
                        i.then_inc(av_done, 1)
                        if t < NT - 1:
                            pe.wait_ge(kg_ready, t + 1)
                            for h in range(NH):
                                r = (h % 2) * DH
                                c0 = (6 + t % 2) * BANK + (h // 2) * D1
                                i = nc.tensor.matmul(PS[r:r + DH, c0:c0 + D1], kt[:, t, h * DH:(h + 1) * DH],
                                                     v1[:, t, h, :], start=True, stop=True)
                            i.then_inc(u_done, 1)

                @block.gpsimd
                def _(pool):
                    for t in range(NT - 1):
                        k = kt[:, t, :].rearrange("p (h d) -> p h d", d=DH)
                        nc.gpsimd.tensor_tensor(k, k, tokv[:, 1, t, :].unsqueeze(2).to_broadcast([P, NH, DH]),
                                                ALU.mult).then_inc(kg_ready, 1)

                @block.scalar
                def _(act):
                    for t in range(NT):
                        act.wait_ge(arg_ready, t + 1)
                        for h in range(NH):
                            i = nc.scalar.activation(E[:, t % 2, h, :], E[:, t % 2, h, :], ACT.Exp,
                                                     bias=tokv[:, 0, t, h:h + 1])
                        i.then_inc(e_ready, 1)
                        if t >= 1:
                            act.wait_ge(h_ready, t)
                            nc.scalar.activation(sq[:, :, :], H[:, t - 1, :, :], ACT.Square).then_inc(sq_ready, 1)
                    act.wait_ge(h_ready, NT)
                    nc.scalar.activation(sq[:, :, :], H[:, NT - 1, :, :], ACT.Square).then_inc(sq_ready, 1)

                @block.vector
                def _(dve):
                    def arg(t):
                        dve.wait_ge(cmb_loaded[t % 2], 16 * (t // 2 + 1))
                        if t >= 2:
                            dve.wait_ge(p_ready, t - 1)
                        nc.vector.tensor_tensor(E[:, t % 2, :, :], cmb[:, t % 2, :, :],
                                                causal[:, :].unsqueeze(1).to_broadcast([P, NH, P]),
                                                ALU.add).then_inc(arg_ready, 1)

                    def variance(t):
                        dve.wait_ge(sq_ready, t + 1)
                        vstep(dve, nc.vector.tensor_reduce(var[:, t, :], sq[:, :, :], AX.X, ALU.add))

                    def weights(t):
                        dve.wait_ge(s_ready, t + 1)
                        dve.wait_ge(e_ready, t + 1)
                        if t >= 2:
                            dve.wait_ge(av_done, t - 1)
                        nc.vector.tensor_tensor(by_pair(Pr[:, t % 2, :, :]),
                                                PS[:, (t % 2) * T:(t % 2 + 1) * T].rearrange("p (b a n) -> p a b n", b=2, n=P),
                                                by_pair(E[:, t % 2, :, :]), ALU.mult).then_inc(p_ready, 1)

                    arg(0)
                    arg(1)
                    weights(0)
                    arg(2)
                    for t in range(NT):
                        if t < NT - 1:
                            weights(t + 1)
                        if t + 3 < NT:
                            arg(t + 3)
                        if t < NT - 1:
                            dve.wait_ge(u_done, t + 1)
                            for i in range(IT):
                                c0 = (6 + t % 2) * BANK + i * D1
                                u = PS[:, c0:c0 + D1]
                                if t == 0:
                                    m = nc.vector.tensor_copy(state[:, i, :], u)
                                else:
                                    m = nc.vector.scalar_tensor_tensor(state[:, i, :], state[:, i, :], fade[:, i, t:t + 1],
                                                                       u, ALU.mult, ALU.add)
                            m.then_inc(state_ready, 1)
                        dve.wait_ge(av_done, t + 1)
                        o = o_all()
                        vstep(dve, nc.vector.tensor_copy(den[:, :].rearrange("p (a b) -> p a b", b=2), o[:, :, :, DH]))
                        vstep(dve, nc.vector.scalar_tensor_tensor(nrm[:, :], den[:, :], -1.0, den[:, :], ALU.mult, ALU.max))
                        vstep(dve, nc.vector.tensor_tensor(nrm[:, :], nrm[:, :], tokv[:, 2, t, :], ALU.max))
                        vstep(dve, nc.vector.tensor_scalar(nrm[:, :], nrm[:, :], 1e-6, None, ALU.add))
                        vstep(dve, nc.vector.reciprocal(den[:, :], nrm[:, :]))
                        nc.vector.tensor_tensor(by_pair(H[:, t, :, :]), o[:, :, :, 0:DH],
                                                by_pair(den[:, :].unsqueeze(2)).to_broadcast([P, NH // 2, 2, DH]),
                                                ALU.mult).then_inc(o_used, 1)
                        dve.wait_ge(o_used, t + 1)
                        vstep(dve, nc.vector.tensor_reduce(mu[:, :], H[:, t, :, :], AX.X, ALU.add))
                        vstep(dve, nc.vector.tensor_scalar(mu[:, :], mu[:, :], 1.0 / DH, None, ALU.mult))
                        if t >= 1:
                            variance(t - 1)
                        nc.vector.tensor_tensor(H[:, t, :, :], H[:, t, :, :], mu[:, :].unsqueeze(2).to_broadcast([P, NH, DH]),
                                                ALU.subtract).then_inc(h_ready, 1)
                    variance(NT - 1)
                    vstep(dve, nc.vector.tensor_scalar(var[:, :, :], var[:, :, :], 1.0 / DH, 1e-5, ALU.mult, ALU.add))

            with nc.Block() as block:
                @block.scalar
                def _(act):
                    nc.scalar.activation(rstd[:, :, :], var[:, :, :], ACT.Sqrt).then_inc(sd_ready, 1)
                    for i in range(IT):
                        nc.scalar.activation(xa[:, i, :], xa[:, i, :], ACT.Copy,
                                             scale=cols[:, 2, i:i + 1]).then_inc(skip_ready, 1)

                @block.vector
                def _(dve):
                    dve.wait_ge(sd_ready, 1)
                    vstep(dve, nc.vector.reciprocal(var[:, :, :], rstd[:, :, :]))
                    for t in range(NT):
                        nc.vector.tensor_tensor(H[:, t, :, :], H[:, t, :, :], var[:, t, :].unsqueeze(2).to_broadcast([P, NH, DH]),
                                                ALU.mult).then_inc(h_scaled, 1)
                    for i in range(IT):
                        dve.wait_ge(h_turned, i + 1)
                        dve.wait_ge(skip_ready, i + 1)
                        vstep(dve, nc.vector.scalar_tensor_tensor(hT[:, i, :], PS[:, i * T:(i + 1) * T], cols[:, 1, i:i + 1],
                                                                  xa[:, i, :], ALU.mult, ALU.add))
                        nc.vector.tensor_tensor(hT[:, i, :], hT[:, i, :], sz[:, i, :], ALU.mult).then_inc(h_done, 1)
                    for k in range(2 * HALVES):
                        dve.wait_ge(out_done, k + 1)
                        s = slice((k % 2) * BANK, (k % 2 + 1) * BANK)
                        nc.vector.tensor_tensor(xT[:, k // 2, s], xT[:, k // 2, s], PS[:, k * BANK:(k + 1) * BANK],
                                                ALU.add).then_inc(added, 1)

                @block.tensor
                def _(pe):
                    pe.wait_ge(h_scaled, NT)
                    for i in range(IT):
                        for t in range(NT):
                            src = H[:, t, 2 * i:2 * i + 2, :].rearrange("p h d -> p (h d)")
                            m = nc.tensor.transpose(PS[:, i * T + t * P:i * T + (t + 1) * P], src, ident[:, :])
                        m.then_inc(h_turned, 1)
                    pe.wait_ge(h_done, IT)
                    for k in range(2 * HALVES):
                        project(nc, PS[:, k * BANK:(k + 1) * BANK], wdn, hT, k // 2, (k % 2) * BANK,
                                (k % 2 + 1) * BANK).then_inc(out_done, 1)

                @block.sync
                def _(sp):
                    sp.wait_ge(added, 2 * HALVES)
                    sp.dma_start(y[b, :, :, :], xT[:, :, :]).then_inc(stored, 16)
                    sp.wait_ge(stored, 16)
            L.barrier_and_clear()
            vstep.restart()
            astep.restart()


class Window:

    def __init__(self, L, width, soft):
        self.logits = L.sb("logits", [P, 3, width])
        self.PT = L.sb("PT", [P, 2, 3 * P])
        self.low = L.sb("low", [P, 4])
        self.total = L.sb("total", [P, 4])
        self.inv = L.sb("inv", [P, 4])
        self.s_ready = L.sem("s_ready")
        self.l_ready = L.sem("l_ready")
        self.e_ready = L.sem("e_ready")
        self.inv_ready = L.sem("inv_ready")
        self.p_ready = L.sem("p_ready")
        self.turned = L.sem("turned")
        self.pt_ready = L.sem("pt_ready")
        self.pt_used = L.sem("pt_used")
        self.o_copied = L.sem("o_copied")
        if soft:
            self.soft = L.sb("soft", [P, 2, width])
            self.soft_ready = L.sem("soft_ready")


def window_attention(nc, PS, w, split, qk, qk_ready, V, OT, ident, table, offs, widths, before, soft=None):
    UNITS = NT * NH
    with nc.Block() as block:
        @block.sync
        def _(sp):
            split.sync(nc, sp, w.s_ready)

        if soft is not None:
            @block.gpsimd
            def _(pool):
                before.gpsimd(pool)

        @block.tensor
        def _(pe):
            def scores(n):
                h, t = n // NT, n % NT
                k0, k1 = key_blocks(t)
                slot, c0 = h % split.SLOTS, (n % 3) * BANK
                if t == 0:
                    split.wait(pe, h)
                if n >= 3:
                    pe.wait_ge(w.l_ready, n - 2)
                if soft is not None:
                    cls = tile_class(t)
                    nc.tensor.matmul(PS[:, c0:c0 + widths[cls]], soft[0], soft[1][:, offs[cls]:offs[cls] + widths[cls]],
                                     start=True, stop=False)
                for e in range(2):
                    i = nc.tensor.matmul(PS[:, c0:c0 + (k1 - k0) * P], split.q[:, slot, e, t * P:(t + 1) * P],
                                         split.k[:, slot, e, k0 * P:k1 * P], start=(soft is None and e == 0), stop=(e == 1))
                i.then_inc(w.s_ready, 1)

            def turn(n):
                k0, k1 = key_blocks(n % NT)
                pe.wait_ge(w.p_ready, n + 1)
                if n >= 2:
                    pe.wait_ge(w.pt_ready, n - 1)
                for j in range(k1 - k0):
                    c0 = (3 + n % 2) * BANK + j * P
                    i = nc.tensor.transpose(PS[:, c0:c0 + P], w.logits[:, n % 3, j * P:(j + 1) * P], ident[:, :])
                i.then_inc(w.turned, 1)

            def weigh(n):
                h, t = n // NT, n % NT
                k0, k1 = key_blocks(t)
                pe.wait_ge(w.pt_ready, n + 1)
                if t == 0 and h >= 4:
                    pe.wait_ge(w.o_copied, h - 3)
                r, c0 = (h % 4) * HD, 5 * BANK + t * P
                for j in range(k1 - k0):
                    i = nc.tensor.matmul(PS[r:r + HD, c0:c0 + P], V[:, k0 + j, h * HD:(h + 1) * HD],
                                         w.PT[:, n % 2, j * P:(j + 1) * P], start=(j == 0), stop=(j == k1 - k0 - 1))
                i.then_inc(w.pt_used, 1)

            before.tensor(pe)
            for n in range(UNITS + 3):
                if n < UNITS:
                    scores(n)
                if 0 <= n - 2 < UNITS:
                    turn(n - 2)
                if n >= 3:
                    weigh(n - 3)

        @block.vector
        def _(dve):
            def normalise(n):
                k0, k1 = key_blocks(n % NT)
                dve.wait_ge(w.e_ready, n + 1)
                nc.vector.reciprocal(w.inv[:, n % 4:n % 4 + 1], w.total[:, n % 4:n % 4 + 1]).then_inc(w.inv_ready, 1)
                dve.wait_ge(w.inv_ready, n + 1)
                p = w.logits[:, n % 3, 0:(k1 - k0) * P]
                nc.vector.tensor_scalar(p, p, w.inv[:, n % 4:n % 4 + 1], None, ALU.mult).then_inc(w.p_ready, 1)

            def copy_turned(n):
                k0, k1 = key_blocks(n % NT)
                dve.wait_ge(w.turned, n + 1)
                if n >= 2:
                    dve.wait_ge(w.pt_used, n - 1)
                nk = (k1 - k0) * P
                nc.vector.tensor_copy(w.PT[:, n % 2, 0:nk],
                                      PS[:, (3 + n % 2) * BANK:(3 + n % 2) * BANK + nk]).then_inc(w.pt_ready, 1)

            before.vector(dve)
            split.vector(nc, dve, qk, [1])
            for n in range(UNITS + 2):
                if n < UNITS:
                    h, t = n // NT, n % NT
                    cls = tile_class(t)
                    W = widths[cls]
                    c0 = (n % 3) * BANK
                    dve.wait_ge(w.s_ready, n + 1)
                    if soft is not None:
                        dve.wait_ge(w.soft_ready, n + 1)
                        add, gain = w.soft[:, n % 2, 0:W], soft[4]
                    else:
                        add, gain = table[:, h, offs[cls]:offs[cls] + W], 1.0
                    if n >= 3:
                        dve.wait_ge(w.turned, n - 2)
                    nc.vector.tensor_tensor_reduce(out=w.logits[:, n % 3, 0:W], in0=PS[:, c0:c0 + W], in1=add, scale=-gain,
                                                   scalar=3.0e38, op0=ALU.add, op1=ALU.min,
                                                   accum_out=w.low[:, n % 4:n % 4 + 1]).then_inc(w.l_ready, 1)
                if 0 <= n - 1 < UNITS:
                    normalise(n - 1)
                if n >= 2 and soft is not None:
                    copy_turned(n - 2)

        @block.scalar
        def _(act):
            def soften(n):
                h, t = n // NT, n % NT
                cls = tile_class(t)
                W = widths[cls]
                if n >= 2:
                    act.wait_ge(w.l_ready, n - 1)
                nc.scalar.activation(w.soft[:, n % 2, 0:W], table[:, offs[cls]:offs[cls] + W], ACT.Tanh,
                                     bias=soft[3][:, t, h:h + 1], scale=soft[2][:, t, h:h + 1]).then_inc(w.soft_ready, 1)

            def copy_turned(n):
                k0, k1 = key_blocks(n % NT)
                act.wait_ge(w.turned, n + 1)
                if n >= 2:
                    act.wait_ge(w.pt_used, n - 1)
                nk = (k1 - k0) * P
                nc.scalar.activation(w.PT[:, n % 2, 0:nk], PS[:, (3 + n % 2) * BANK:(3 + n % 2) * BANK + nk],
                                     ACT.Copy).then_inc(w.pt_ready, 1)

            def copy_out(h):
                act.wait_ge(w.pt_used, NT * (h + 1))
                r = (h % 4) * HD
                nc.scalar.activation(OT[r:r + HD, h // 4, :], PS[r:r + HD, 5 * BANK:7 * BANK],
                                     ACT.Copy).then_inc(w.o_copied, 1)

            before.scalar(act)
            split.scalar(nc, act, qk, qk_ready)
            if soft is not None:
                soften(0)
            for n in range(UNITS + 2):
                if soft is not None and n + 1 < UNITS:
                    soften(n + 1)
                if n < UNITS:
                    W = widths[tile_class(n % NT)]
                    act.wait_ge(w.l_ready, n + 1)
                    e = w.logits[:, n % 3, 0:W]
                    nc.scalar.activation(e, e, ACT.Exp, scale=-1.0, bias=w.low[:, n % 4:n % 4 + 1],
                                         accum_out=w.total[:, n % 4:n % 4 + 1]).then_inc(w.e_ready, 1)
                if n >= 2 and soft is None:
                    copy_turned(n - 2)
                if n >= NT + 4 and (n - 4) % NT == 0:
                    copy_out((n - 4) // NT - 1)
            copy_out(NH - 1)


WINDOW_W = (2 * P, 3 * P, 2 * P)
WINDOW_O = (0, 2 * P, 5 * P)


def layer2(nc, A, x, y, skew):
    with ExitStack() as ctx:
        L = Layer(nc, ctx, "l2")
        vstep = Chain(L.sem("vstep"))
        g = Norm(L, vstep)
        PS = L.ps
        W = sum(WINDOW_W)
        wqkv = L.sb("w_qkv", [P, HALVES, 3 * C])
        wo = L.sb("w_proj", [P, HALVES, C])
        ident = L.sb("ident", [P, P])
        qkv_b = L.sb("qkv_b", [P, 3 * HALVES])
        v_b = L.sb("v_b", [P, C])
        proj_b = L.sb("proj_b", [P, HALVES])
        bias = L.sb("bias", [P, NH, W])
        window = L.sb("window", [P, W])
        xT = L.sb("xT", [P, HALVES, T])
        xn = L.sb("xn", [P, HALVES, T])
        qk = L.sb("qk", [P, 2 * HALVES, T])
        V = L.sb("V", [P, NT, C])
        OT = L.sb("OT", [P, HALVES, T])
        w = Window(L, max(WINDOW_W), False)
        split = Split(L)
        proj_done, qk_copied, v_done, v_copied = L.sem("proj_done"), L.sem("qk_copied"), L.sem("v_done"), L.sem("v_copied")
        out_done, added, stored = L.sem("out_done"), L.sem("added"), L.sem("stored")
        spread, skewed = L.sem("spread"), L.sem("skewed")

        load_all(nc, L, [
            (wqkv[:, :, :], A["L2_WqkvT"].rearrange("(k p) n -> p k n", k=HALVES)),
            (wo[:, :, :], A["L2_WprojT"].rearrange("(k p) n -> p k n", k=HALVES)),
            (ident[:, :], A["ident"]), (g.group_mean[:, :], A["group_mean"]), (window[:, :], A["window"]),
            (qkv_b[:, :], A["L2_qkv_b"]), (proj_b[:, :], A["L2_proj_b"]),
            (v_b[:, :], A["L2_v_b"].partition_broadcast(P)),
        ])
        with nc.Block() as block:
            rows, width = WIN * 2 - 1 + sum(RPB_ROWS), 2 * SIDE - 1
            head, size = rows * width, NH * rows * width
            first_row = (WIN - 1 + RPB_ROWS[0], WIN - 1 + RPB_ROWS[0] - ROWS, WIN - 1 + RPB_ROWS[0] - ROWS)

            @block.sync
            def _(sp):
                sp.dma_start(skew, A["L2_rpb"].rearrange("h r c -> (h r c)").partition_broadcast(SIDE)).then_inc(spread, 16)
                sp.wait_ge(spread, 16)
                n = 0
                for cls in range(3):
                    for qr in range(ROWS):
                        for h in range(NH):
                            src = bass.AP(skew.tensor, h * head + (first_row[cls] - qr) * width + SIDE - 1,
                                          [[size - 1, SIDE], [width, WINDOW_W[cls] // SIDE], [1, SIDE]])
                            dst = bias[qr * SIDE:(qr + 1) * SIDE, h, WINDOW_O[cls]:WINDOW_O[cls] + WINDOW_W[cls]]
                            sp.dma_start(dst.rearrange("p (r c) -> p r c", c=SIDE), src).then_inc(skewed, 16)
                            n += 1
                sp.wait_ge(skewed, 16 * n)

            @block.vector
            def _(dve):
                dve.wait_ge(skewed, 16 * 3 * ROWS * NH)
                for h in range(NH):
                    nc.vector.tensor_tensor(bias[:, h, :], bias[:, h, :], window[:, :], ALU.add)
                vstep(dve, nc.vector.tensor_scalar(qkv_b[:, 0:HALVES], qkv_b[:, 0:HALVES], HD ** -0.5, None, ALU.mult))
        L.barrier_and_clear()
        vstep.restart()

        with nc.Fori(0, B) as b:
            groupnorm(nc, L, g, xT, xn, PS, b, load=x)

            class before:
                def tensor(pe):
                    for u in range(2 * HALVES):
                        for n in range(2):
                            i = project(nc, PS[:, u * T + n * BANK:u * T + (n + 1) * BANK], wqkv, xn, u,
                                        n * BANK, (n + 1) * BANK)
                        i.then_inc(proj_done, 1)
                    for t in range(NT):
                        if t == 0:
                            pe.wait_ge(qk_copied, 2)
                        i = project_tokens(nc, PS[:, t * C:(t + 1) * C], xn, wqkv[:, :, 2 * C:3 * C], t)
                        if t % 2 == 1:
                            i.then_inc(v_done, 1)
                    pe.wait_ge(qk_copied, 2 * HALVES)
                    pe.wait_ge(v_copied, NT // 2)

                def scalar(act):
                    for u in range(2 * HALVES):
                        act.wait_ge(proj_done, u + 1)
                        nc.scalar.activation(qk[:, u, :], PS[:, u * T:(u + 1) * T], ACT.Identity, bias=qkv_b[:, u:u + 1],
                                             scale=HD ** -0.5 if u < HALVES else 1.0).then_inc(qk_copied, 1)

                def vector(dve):
                    split.vector(nc, dve, qk, [0])
                    for k in range(NT // 2):
                        dve.wait_ge(v_done, k + 1)
                        nc.vector.tensor_tensor(V[:, 2 * k:2 * k + 2, :],
                                                PS[:, k * BANK:(k + 1) * BANK].rearrange("p (t c) -> p t c", t=2),
                                                v_b[:, :].unsqueeze(1).to_broadcast([P, 2, C]), ALU.add).then_inc(v_copied, 1)

            window_attention(nc, PS, w, split, qk, qk_copied, V, OT, ident, bias, WINDOW_O, WINDOW_W, before)

            with nc.Block() as block:
                @block.tensor
                def _(pe):
                    for k in range(2 * HALVES):
                        project(nc, PS[:, k * BANK:(k + 1) * BANK], wo, OT, k // 2, (k % 2) * BANK,
                                (k % 2 + 1) * BANK).then_inc(out_done, 1)

                @block.vector
                def _(dve):
                    for k in range(2 * HALVES):
                        dve.wait_ge(out_done, k + 1)
                        s = slice((k % 2) * BANK, (k % 2 + 1) * BANK)
                        nc.vector.scalar_tensor_tensor(xT[:, k // 2, s], PS[:, k * BANK:(k + 1) * BANK],
                                                       proj_b[:, k // 2:k // 2 + 1], xT[:, k // 2, s],
                                                       ALU.add, ALU.add).then_inc(added, 1)

                @block.sync
                def _(sp):
                    sp.wait_ge(added, 2 * HALVES)
                    sp.dma_start(y[b, :, :, :], xT[:, :, :]).then_inc(stored, 16)
                    sp.wait_ge(stored, 16)
            L.barrier_and_clear()
            vstep.restart()


SOFT_W = tuple(w + p for w, p in zip(WINDOW_W, PADS))
SOFT_O = (0, SOFT_W[0], SOFT_W[0] + SOFT_W[1])
SHARPNESS = 10000.0


def layer3(nc, A, x, out):
    with ExitStack() as ctx:
        L = Layer(nc, ctx, "l3")
        vstep = Chain(L.sem("vstep"))
        g = Norm(L, vstep)
        PS = L.ps
        W = sum(SOFT_W)
        GAIN = SHARPNESS / 2
        MAXD = float(np.sqrt(2.0) * (WIN // 2))
        wqkv = L.sb("w_qkv", [P, HALVES, 3 * C])
        wo = L.sb("w_out", [P, HALVES, C])
        wwp = L.sb("w_wp", [P, HALVES, 2 * NH])
        b_wp = L.sb("b_wp", [P, 2 * NH])
        w_on = L.sb("w_on", [P, HALVES])
        w_qk = L.sb("w_qk", [P, 2])
        ident = L.sb("ident", [P, P])
        identb = L.sb("identb", [P, P], BF16)
        head_mean = L.sb("head_mean", [P, P])
        all_mean = L.sb("all_mean", [P, P])
        dist = L.sb("dist", [P, W])
        outside = L.sb("outside", [P, W], BF16)
        eps = L.sb("eps", [P, 1])
        xT = L.sb("xT", [P, HALVES, T])
        xn = L.sb("xn", [P, HALVES, T])
        qk = L.sb("qk", [P, 2 * HALVES, T])
        square = L.sb("square", [P, 2 * HALVES, T])
        rec = L.sb("rec", [P, 2, T])
        V = L.sb("V", [P, NT, C])
        VT = L.sb("VT", [P, HALVES, T])
        OT = L.sb("OT", [P, HALVES, T])
        xo = L.sb("xo", [P, NT, C])
        wp = L.sb("wp", [P, NT, 2 * NH])
        sharp = L.sb("sharp", [P, NT, NH])
        edge = L.sb("edge", [P, NT, NH])
        w = Window(L, max(SOFT_W), True)
        split = Split(L)
        proj_done, qk_copied, v_done, v_copied = L.sem("proj_done"), L.sem("qk_copied"), L.sem("v_done"), L.sem("v_copied")
        wp_done, wp_biased, wp_silu, wp_tanh = L.sem("wp_done"), L.sem("wp_biased"), L.sem("wp_silu"), L.sem("wp_tanh")
        squared, mean_ready, root_ready, qk_normed = L.sem("squared"), L.sem("mean_ready"), L.sem("root_ready"), L.sem("qk_normed")
        o_squared, o_mean, o_root, o_ready = L.sem("o_squared"), L.sem("o_mean"), L.sem("o_root"), L.sem("o_ready")
        out_done, out_silu, added, turned = L.sem("out_done"), L.sem("out_silu"), L.sem("added"), L.sem("x_turned")
        log_ready, o_log = L.sem("log_ready"), L.sem("o_log")
        x_copied, stored, vt_done, vt_copied = L.sem("x_copied"), L.sem("stored"), L.sem("vt_done"), L.sem("vt_copied")

        load_all(nc, L, [
            (wqkv[:, :, :], A["L3_WqkvT"].rearrange("(k p) n -> p k n", k=HALVES)),
            (wo[:, :, :], A["L3_WoutT"].rearrange("(k p) n -> p k n", k=HALVES)),
            (wwp[:, :, :], A["L3_WwpT"].rearrange("(k p) n -> p k n", k=HALVES)),
            (ident[:, :], A["ident"]), (g.group_mean[:, :], A["group_mean"]), (head_mean[:, :], A["head_mean"]),
            (dist[:, :], A["dist"]), (square[:, :, :].rearrange("p k n -> p (k n)")[:, 0:W], A["outside"]),
            (w_qk[:, :], A["L3_w_qk"]), (w_on[:, :], A["L3_w_on"]),
            (b_wp[:, :], A["L3_b_wp"].partition_broadcast(P)),
        ])
        with nc.Block() as block:
            @block.vector
            def _(dve):
                nc.vector.memset(eps[:, :], 1e-6)
                nc.vector.memset(all_mean[:, :], 1.0 / C)
                nc.vector.tensor_copy(identb[:, :], ident[:, :])
                nc.vector.tensor_scalar(w_qk[:, 0:1], w_qk[:, 0:1], HD ** -0.5 / GAIN, None, ALU.mult)
                vstep(dve, nc.vector.tensor_copy(outside[:, :], square[:, :, :].rearrange("p k n -> p (k n)")[:, 0:W]))
        L.barrier_and_clear()
        vstep.restart()

        with nc.Fori(0, B) as b:
            groupnorm(nc, L, g, xT, xn, PS, b, load=x)

            class before:
                def tensor(pe):
                    for u in range(3):
                        for n in range(2):
                            i = project(nc, PS[:, u * T + n * BANK:u * T + (n + 1) * BANK], wqkv, xn, u,
                                        n * BANK, (n + 1) * BANK)
                        i.then_inc(proj_done, 1)
                    for t in range(NT):
                        i = project_tokens(nc, PS[:, 7 * BANK + t * 2 * NH:7 * BANK + (t + 1) * 2 * NH], xn, wwp, t)
                    i.then_inc(wp_done, 1)
                    pe.wait_ge(qk_copied, 1)
                    for n in range(2):
                        i = project(nc, PS[:, n * BANK:(n + 1) * BANK], wqkv, xn, 3, n * BANK, (n + 1) * BANK)
                    i.then_inc(proj_done, 1)
                    for t in range(NT):
                        if t == 0:
                            pe.wait_ge(qk_copied, 3)
                        c0 = 2 * BANK + t * C
                        i = project_tokens(nc, PS[:, c0:c0 + C], xn, wqkv[:, :, 2 * C:3 * C], t)
                        if t % 2 == 1:
                            i.then_inc(v_done, 1)
                    for u in range(2 * HALVES):
                        pe.wait_ge(squared, u + 1)
                        if u == 0:
                            pe.wait_ge(qk_copied, 4)
                        elif u == 1:
                            pe.wait_ge(v_copied, 2)
                        elif u == 2:
                            pe.wait_ge(v_copied, 4)
                        else:
                            pe.wait_ge(log_ready, 1)
                        c0 = (u % 3) * T
                        for n in range(2):
                            i = nc.tensor.matmul(PS[:, c0 + n * BANK:c0 + (n + 1) * BANK], head_mean[:, :],
                                                 square[:, u, n * BANK:(n + 1) * BANK], start=True, stop=True)
                        i.then_inc(mean_ready, 1)
                    for k in range(2 * HALVES):
                        c0 = (6 + k % 2) * BANK
                        pe.wait_ge(wp_biased, 1)
                        if k >= 2:
                            pe.wait_ge(vt_copied, k - 1)
                        for j in range(4):
                            t = (k % 2) * 4 + j
                            i = nc.tensor.transpose(PS[:, c0 + j * P:c0 + (j + 1) * P], V[:, t, (k // 2) * P:(k // 2 + 1) * P],
                                                    ident[:, :])
                        i.then_inc(vt_done, 1)
                    pe.wait_ge(log_ready, 2 * HALVES)
                    pe.wait_ge(vt_copied, 2 * HALVES)

                def scalar(act):
                    for u in range(2 * HALVES):
                        act.wait_ge(proj_done, u + 1)
                        nc.scalar.activation(qk[:, u, :], PS[:, (u % 3) * T:(u % 3 + 1) * T], ACT.Silu).then_inc(qk_copied, 1)
                    act.wait_ge(wp_biased, 1)
                    nc.scalar.activation(wp[:, :, :], wp[:, :, :], ACT.Silu).then_inc(wp_silu, 1)
                    for k in range(NT // 2):
                        act.wait_ge(v_done, k + 1)
                        nc.scalar.activation(V[:, 2 * k:2 * k + 2, :].rearrange("p t c -> p (t c)"),
                                             PS[:, (2 + k) * BANK:(3 + k) * BANK], ACT.Silu).then_inc(v_copied, 1)
                    act.wait_ge(wp_silu, 1)
                    nc.scalar.activation(wp[:, :, :], wp[:, :, :], ACT.Tanh, scale=0.5).then_inc(wp_tanh, 1)
                    for pair in ((0, 1), (2, 3)):
                        for u in pair:
                            act.wait_ge(mean_ready, u + 1)
                            if u >= 2:
                                act.wait_ge(qk_normed, u - 1)
                            nc.scalar.activation(rec[:, u % 2, :], PS[:, (u % 3) * T:(u % 3 + 1) * T], ACT.Ln,
                                                 bias=eps[:, :]).then_inc(log_ready, 1)
                        for u in pair:
                            act.wait_ge(log_ready, u + 1)
                            nc.scalar.activation(rec[:, u % 2, :], rec[:, u % 2, :], ACT.Exp,
                                                 scale=-0.5).then_inc(root_ready, 1)
                    for k in range(2 * HALVES):
                        act.wait_ge(vt_done, k + 1)
                        nc.scalar.activation(VT[:, k // 2, (k % 2) * BANK:(k % 2 + 1) * BANK],
                                             PS[:, (6 + k % 2) * BANK:(7 + k % 2) * BANK], ACT.Copy).then_inc(vt_copied, 1)

                def gpsimd(pool):
                    for u in range(2 * HALVES):
                        pool.wait_ge(qk_copied, u + 1)
                        nc.gpsimd.tensor_tensor(square[:, u, :], qk[:, u, :], qk[:, u, :], ALU.mult).then_inc(squared, 1)

                def vector(dve):
                    dve.wait_ge(wp_done, 1)
                    nc.vector.tensor_tensor(wp[:, :, :], PS[:, 7 * BANK:7 * BANK + NT * 2 * NH].rearrange(
                        "p (t c) -> p t c", t=NT), b_wp[:, :].unsqueeze(1).to_broadcast([P, NT, 2 * NH]),
                        ALU.add).then_inc(wp_biased, 1)
                    dve.wait_ge(wp_tanh, 1)
                    vstep(dve, nc.vector.tensor_scalar(edge[:, :, :], wp[:, :, 0:NH], MAXD / 2, MAXD / 2 + 0.5, ALU.mult, ALU.add))
                    vstep(dve, nc.vector.tensor_scalar(sharp[:, :, :], wp[:, :, NH:2 * NH], -9.5 / 4, -(9.5 / 2 + 0.5) / 2,
                                                       ALU.mult, ALU.add))
                    vstep(dve, nc.vector.scalar_tensor_tensor(edge[:, :, :], edge[:, :, :], -1.0, sharp[:, :, :],
                                                              ALU.mult, ALU.mult))
                    for u in range(2 * HALVES):
                        dve.wait_ge(root_ready, u + 1)
                        s = u // HALVES
                        nc.vector.scalar_tensor_tensor(qk[:, u, :], rec[:, u % 2, :], w_qk[:, s:s + 1], qk[:, u, :],
                                                       ALU.mult, ALU.mult).then_inc(qk_normed, 1)
                    split.vector(nc, dve, qk, [0])

            window_attention(nc, PS, w, split, qk, qk_normed, V, OT, ident, dist, SOFT_O, SOFT_W, before,
                             soft=(identb[:, :], outside, sharp, edge, GAIN))

            with nc.Block() as block:
                @block.tensor
                def _(pe):
                    pe.wait_ge(o_squared, HALVES)
                    for n in range(2):
                        for k in range(HALVES):
                            i = nc.tensor.matmul(PS[:, n * BANK:(n + 1) * BANK], all_mean[:, :],
                                                 square[:, k, n * BANK:(n + 1) * BANK], start=(k == 0), stop=(k == HALVES - 1))
                    i.then_inc(o_mean, 1)
                    pe.wait_ge(o_ready, HALVES)
                    for k in range(2 * HALVES):
                        project(nc, PS[:, (4 + k) * BANK:(5 + k) * BANK], wo, OT, k // 2, (k % 2) * BANK,
                                (k % 2 + 1) * BANK).then_inc(out_done, 1)
                    for k in range(2 * HALVES):
                        pe.wait_ge(added, 2 * HALVES)
                        for j in range(4):
                            t, hf = 2 * k + j // 2, j % 2
                            i = nc.tensor.transpose(PS[:, k * BANK + j * P:k * BANK + (j + 1) * P],
                                                    xT[:, hf, t * P:(t + 1) * P], ident[:, :])
                        i.then_inc(turned, 1)

                @block.scalar
                def _(act):
                    for k in range(HALVES):
                        nc.scalar.activation(square[:, k, :], OT[:, k, :], ACT.Square).then_inc(o_squared, 1)
                    act.wait_ge(o_mean, 1)
                    nc.scalar.activation(rec[:, 0, :], PS[:, 0:T], ACT.Ln, bias=eps[:, :]).then_inc(o_log, 1)
                    act.wait_ge(o_log, 1)
                    nc.scalar.activation(rec[:, 1, :], rec[:, 0, :], ACT.Exp, scale=-0.5).then_inc(o_root, 1)
                    for k in range(2 * HALVES):
                        act.wait_ge(out_done, k + 1)
                        nc.scalar.activation(square[:, k // 2, (k % 2) * BANK:(k % 2 + 1) * BANK],
                                             PS[:, (4 + k) * BANK:(5 + k) * BANK], ACT.Silu).then_inc(out_silu, 1)
                    for k in (1, 3):
                        act.wait_ge(turned, k + 1)
                        nc.scalar.activation(xo[:, 2 * k:2 * k + 2, :].rearrange("p t c -> p (t c)"),
                                             PS[:, k * BANK:(k + 1) * BANK], ACT.Copy).then_inc(x_copied, 1)

                @block.vector
                def _(dve):
                    dve.wait_ge(o_root, 1)
                    for k in range(HALVES):
                        vstep(dve, nc.vector.scalar_tensor_tensor(OT[:, k, :], OT[:, k, :], w_on[:, k:k + 1], rec[:, 1, :],
                                                                  ALU.mult, ALU.mult))
                        nc.vector.tensor_tensor(OT[:, k, :], OT[:, k, :], VT[:, k, :], ALU.add).then_inc(o_ready, 1)
                    for k in range(2 * HALVES):
                        dve.wait_ge(out_silu, k + 1)
                        s = slice((k % 2) * BANK, (k % 2 + 1) * BANK)
                        nc.vector.tensor_tensor(xT[:, k // 2, s], xT[:, k // 2, s], square[:, k // 2, s],
                                                ALU.add).then_inc(added, 1)
                    for k in (0, 2):
                        dve.wait_ge(turned, k + 1)
                        nc.vector.tensor_copy(xo[:, 2 * k:2 * k + 2, :].rearrange("p t c -> p (t c)"),
                                              PS[:, k * BANK:(k + 1) * BANK]).then_inc(x_copied, 1)

                @block.sync
                def _(sp):
                    sp.wait_ge(x_copied, 4)
                    for t2 in range(2):
                        dst = out[b, t2 * SIDE // 2:(t2 + 1) * SIDE // 2, :, :].rearrange("(t r) w c -> (r w) t c", r=ROWS)
                        sp.dma_start(dst, xo[:, t2 * 4:t2 * 4 + 4, :]).then_inc(stored, 16)
                    sp.wait_ge(stored, 32)
            L.barrier_and_clear()
            vstep.restart()


def build(nc, A):
    out = nc.dram_tensor("out", (B, SIDE, SIDE, C), F32, kind="ExternalOutput").ap()
    scratch = nc.dram_tensor("scratch", (NH, T), F32, kind="Internal").ap()
    skew = nc.dram_tensor("skew", (SIDE, NH * (2 * WIN - 1 + sum(RPB_ROWS)) * (2 * SIDE - 1)), F32, kind="Internal").ap()
    y0, y1, y2 = (nc.dram_tensor(n, (B, P, HALVES, T), F32, kind="Internal").ap() for n in ("y0", "y1", "y2"))
    layer0(nc, A, A["x"], y0)
    layer1(nc, A, y0, y1, scratch)
    layer2(nc, A, y1, y2, skew)
    layer3(nc, A, y2, out)


def kernel(**inputs):
    import numpy as _np
    import concourse.bacc as _bacc
    from concourse import mybir as _mybir
    from concourse.bass_utils import run_bass_kernel_spmd as _run

    nc = _bacc.Bacc("TRN2", target_bir_lowering=False, num_devices=1)
    i = {k: _np.asarray(v) for k, v in inputs.items()}
    arrays = {"x": i["x"]}
    for n in ("Wq", "Wk", "Wv", "Wo"):
        arrays[f"L0_{n}T"] = i[f"L0_conv_{n}"].T
    for n in ("ln_g", "ln_b"):
        arrays[f"L0_{n}"] = _np.tile(i[f"L0_conv_{n}"], P // HD)[:, None]
    arrays["L1_WupT"] = i["L1_conv_W_up"].T
    arrays["L1_WdownT"] = i["L1_conv_W_down"].T
    fwd = _np.zeros((3, IT, P // 4, 4, P // 4, 4), _np.float32)
    for s, n in enumerate(("Wq", "Wk", "Wv")):
        w = i[f"L1_conv_{n}"].reshape(IT, P // 4, 4, 4)
        for j in range(P // 4):
            fwd[s, :, j, :, j, :] = w[:, j].transpose(0, 2, 1)
    fwd = fwd.reshape(3, IT, P, P)
    arrays["L1_qkv"] = fwd.transpose(2, 0, 1, 3).reshape(P, 3 * IT * P)
    arrays["L1_qkvT"] = fwd.transpose(3, 0, 1, 2).reshape(P, 3 * IT * P)
    gw = _np.zeros((3 * IT, P, 32 + NH), _np.float32)
    gw[:, :, 0:NH] = i["L1_conv_W_i"].T.reshape(3 * IT, P, NH)
    gw[:, :, 32:32 + NH] = i["L1_conv_W_f"].T.reshape(3 * IT, P, NH)
    arrays["L1_gate_w"] = gw.transpose(1, 0, 2).reshape(P, 3 * IT * (32 + NH))
    arrays["L1_conv_w"] = i["L1_conv_conv_w"].reshape(IT, P, TAPS).transpose(1, 0, 2).reshape(P, IT * TAPS)
    cols = _np.stack([i["L1_conv_conv_b"], i["L1_conv_norm_w"], i["L1_conv_skip"]])
    arrays["L1_cols"] = cols.reshape(3, IT, P).transpose(2, 0, 1).reshape(P, 3 * IT)
    arrays["L1_b_i"] = i["L1_conv_b_i"][:, None]
    arrays["L1_b_f"] = i["L1_conv_b_f"][:, None]
    arrays["L2_WqkvT"] = i["L2_conv_qkv_w"].T
    arrays["L2_WprojT"] = i["L2_conv_proj_w"].T
    arrays["L2_qkv_b"] = i["L2_conv_qkv_b"].reshape(3 * HALVES, P).T
    arrays["L2_v_b"] = i["L2_conv_qkv_b"][2 * C:]
    arrays["L2_proj_b"] = i["L2_conv_proj_b"].reshape(HALVES, P).T
    arrays["L2_rpb"] = _np.pad(i["L2_conv_rpb"], ((0, 0), RPB_ROWS, (SIDE - WIN, SIDE - WIN)))
    arrays["L3_WqkvT"] = i["L3_conv_w_qkv"].T
    arrays["L3_WoutT"] = i["L3_conv_w_out"].T
    arrays["L3_WwpT"] = i["L3_conv_w_wp"].T
    arrays["L3_b_wp"] = i["L3_conv_b_wp"]
    arrays["L3_w_on"] = i["L3_conv_w_on"].reshape(HALVES, P).T
    arrays["L3_w_qk"] = _np.stack([_np.tile(i["L3_conv_w_qn"], P // HD), _np.tile(i["L3_conv_w_kn"], P // HD)], 1)
    arrays.update(shape_constants())
    arrays = {k: _np.ascontiguousarray(v) for k, v in arrays.items()}
    A = {k: nc.dram_tensor(k, v.shape, _mybir.dt.from_np(v.dtype), kind="ExternalInput").ap() for k, v in arrays.items()}
    build(nc, A)
    r = _run(nc, [arrays], core_ids=[0])
    return r.results[0]["out"]
```
